# Optimizing a Trainium2 kernel written in Bass

```python
import numpy as np
import jax
import jax.numpy as jnp

def _softmax(x, axis=-1):
    return jax.nn.softmax(x, axis=axis)

def _gelu(x):
    return jax.nn.gelu(x, approximate=True)

def _silu(x):
    return jax.nn.silu(x)

def _sigmoid(x):
    return jax.nn.sigmoid(x)

def _layernorm(x, axis=-1, eps=1e-05):
    m = jnp.mean(x, axis=axis, keepdims=True)
    v = jnp.var(x, axis=axis, keepdims=True)
    return (x - m) / jnp.sqrt(v + eps)

def _scatter_add(tgt, idx, src, axis=0):
    return tgt.at[idx].add(src)

def _segment_sum(src, seg, n):
    return jax.ops.segment_sum(src, seg, n)
kernel_name = 'mk_adaln_d1_jaxref_r4_36916e'

def setup_inputs(seed: int=0):
    np.random.seed(seed)
    _w = jnp.asarray

    def _L0_attn_setup():
        import jax, jax.numpy as jnp
        import numpy as np
        IN_FEATURES = 512
        HEAD_NUM = 64
        D = IN_FEATURES // HEAD_NUM
        SCALE = float(np.sqrt(D))
        key = jax.random.key(seed)
        ks = jax.random.split(key, 9)
        F = IN_FEATURES
        x = jax.random.normal(ks[0], (4, 256, F), dtype=jnp.float32)
        w = lambda k: jax.random.normal(k, (F, F), dtype=jnp.float32) * 0.02
        b = lambda k: jax.random.normal(k, (F,), dtype=jnp.float32) * 0.01
        return {'x': x, 'Wq': w(ks[1]), 'bq': b(ks[2]), 'Wk': w(ks[3]), 'bk': b(ks[4]), 'Wv': w(ks[5]), 'bv': b(ks[6]), 'Wo': w(ks[7]), 'bo': b(ks[8])}
    _L0_attn_in = _L0_attn_setup()

    def _L0_ffn_setup():
        import jax, jax.numpy as jnp
        import numpy as np
        DIM = 512
        HID = 1408
        ZERO_POINT = 128.0

        def _qlinear(x, wq, scale):
            W = (wq.astype(jnp.float32) - ZERO_POINT) * scale[:, None]
            return jnp.einsum('bsd,hd->bsh', x, W)
        key = jax.random.key(seed)
        ks = jax.random.split(key, 7)
        B, S = (4, 512)
        sg = jax.random.uniform(ks[1], (HID,)) * (0.02 / np.sqrt(DIM)) + 0.0001
        su = jax.random.uniform(ks[3], (HID,)) * (0.02 / np.sqrt(DIM)) + 0.0001
        sd = jax.random.uniform(ks[5], (DIM,)) * (0.02 / np.sqrt(HID)) + 0.0001
        return {'x': jax.random.normal(ks[0], (B, S, DIM), dtype=jnp.float32), 'wq_gate': jax.random.randint(ks[2], (HID, DIM), 0, 64, dtype=jnp.int32), 's_gate': sg, 'wq_up': jax.random.randint(ks[4], (HID, DIM), 0, 64, dtype=jnp.int32), 's_up': su, 'wq_down': jax.random.randint(ks[6], (DIM, HID), 0, 64, dtype=jnp.int32), 's_down': sd}
    _L0_ffn_in = _L0_ffn_setup()
    _L0_c = _w((lambda *s: np.random.randn(*s).astype(np.float32) * 0.05)(8, 512))
    _L0_wmod = _w((lambda *s: np.random.randn(*s).astype(np.float32) * 0.05)(512, 6 * 512) * 512 ** (-0.5))
    _d = {'L0_attn_x': _L0_attn_in['x'], 'L0_attn_Wq': _L0_attn_in['Wq'], 'L0_attn_bq': _L0_attn_in['bq'], 'L0_attn_Wk': _L0_attn_in['Wk'], 'L0_attn_bk': _L0_attn_in['bk'], 'L0_attn_Wv': _L0_attn_in['Wv'], 'L0_attn_bv': _L0_attn_in['bv'], 'L0_attn_Wo': _L0_attn_in['Wo'], 'L0_attn_bo': _L0_attn_in['bo'], 'L0_ffn_wq_gate': _L0_ffn_in['wq_gate'], 'L0_ffn_s_gate': _L0_ffn_in['s_gate'], 'L0_ffn_wq_up': _L0_ffn_in['wq_up'], 'L0_ffn_s_up': _L0_ffn_in['s_up'], 'L0_ffn_wq_down': _L0_ffn_in['wq_down'], 'L0_ffn_s_down': _L0_ffn_in['s_down'], 'L0_c': _L0_c, 'L0_wmod': _L0_wmod}
    _x0 = _d['L0_attn_x']
    _d['L0_attn_x'] = jax.random.normal(jax.random.fold_in(jax.random.key(seed), 1), (8, 512, 512), dtype=_x0.dtype)
    del _x0
    return _d

def reference(L0_attn_x, L0_attn_Wq, L0_attn_bq, L0_attn_Wk, L0_attn_bk, L0_attn_Wv, L0_attn_bv, L0_attn_Wo, L0_attn_bo, L0_ffn_wq_gate, L0_ffn_s_gate, L0_ffn_wq_up, L0_ffn_s_up, L0_ffn_wq_down, L0_ffn_s_down, L0_c, L0_wmod):

    def _L0_attn_ref(x, Wq, bq, Wk, bk, Wv, bv, Wo, bo):
        import jax, jax.numpy as jnp
        import numpy as np
        IN_FEATURES = 512
        HEAD_NUM = 64
        D = IN_FEATURES // HEAD_NUM
        SCALE = float(np.sqrt(D))
        B, S, F = x.shape
        d = D
        h = F // d
        q = x @ Wq + bq
        k = x @ Wk + bk
        v = x @ Wv + bv

        def to_heads(t):
            return t.reshape(B, S, d, h).transpose(0, 2, 1, 3)
        q, k, v = (to_heads(q), to_heads(k), to_heads(v))
        scores = jnp.einsum('bdsh,bdth->bdst', q, k) / SCALE
        weights = jax.nn.softmax(scores, axis=-1)
        feats = jnp.einsum('bdst,bdth->bdsh', weights, v)
        feats = feats.transpose(0, 2, 1, 3).reshape(B, S, F)
        return feats @ Wo + bo

    def _L0_ffn_ref(x, wq_gate, s_gate, wq_up, s_up, wq_down, s_down):
        import jax, jax.numpy as jnp
        import numpy as np
        DIM = 512
        HID = 1408
        ZERO_POINT = 128.0

        def _qlinear(x, wq, scale):
            W = (wq.astype(jnp.float32) - ZERO_POINT) * scale[:, None]
            return jnp.einsum('bsd,hd->bsh', x, W)
        gate = _qlinear(x, wq_gate, s_gate)
        gate = jax.nn.silu(gate)
        up = _qlinear(x, wq_up, s_up)
        return _qlinear(gate * up, wq_down, s_down)
    x = L0_attn_x
    mod = (_silu(L0_c) @ L0_wmod).reshape(L0_c.shape[0], 6, 1, -1)
    sa, ca, ga, sb, cb, gb = (mod[:, 0], mod[:, 1], mod[:, 2], mod[:, 3], mod[:, 4], mod[:, 5])
    ga = (2 * (ga >= 0) - 1) * jnp.maximum(jnp.abs(ga), 0.25)
    gb = (2 * (gb >= 0) - 1) * jnp.maximum(jnp.abs(gb), 0.25)
    h = _layernorm(x, axis=-1) * (1 + ca) + sa
    x = x + ga * _L0_attn_ref(h, L0_attn_Wq, L0_attn_bq, L0_attn_Wk, L0_attn_bk, L0_attn_Wv, L0_attn_bv, L0_attn_Wo, L0_attn_bo)
    h = _layernorm(x, axis=-1) * (1 + cb) + sb
    x = x + gb * _L0_ffn_ref(h, L0_ffn_wq_gate, L0_ffn_s_gate, L0_ffn_wq_up, L0_ffn_s_up, L0_ffn_wq_down, L0_ffn_s_down)
    return x

_drawn_inputs = setup_inputs


def setup_inputs(seed=0):
    import zlib

    import numpy as np

    out = dict(_drawn_inputs(seed))
    spreads = {}
    factors = {'L0_attn_Wq': 8.0,
     'L0_attn_bq': 8.0,
     'L0_attn_Wk': 8.0,
     'L0_attn_bk': 64.0,
     'L0_attn_Wv': 8.0,
     'L0_attn_bv': 27.097,
     'L0_attn_Wo': 8.0,
     'L0_attn_bo': 64.0,
     'L0_ffn_s_gate': 8.0,
     'L0_ffn_s_up': 8.0,
     'L0_ffn_s_down': 8.0,
     'L0_c': 4.467,
     'L0_wmod': 4.493}
    for name, (base, spread) in spreads.items():
        noise = np.random.default_rng([zlib.crc32(name.encode()), seed]).standard_normal(out[name].shape)
        drawn = base * np.exp(spread * noise) if base else spread * noise
        out[name] = jnp.asarray(drawn.astype(out[name].dtype))
    for name, factor in factors.items():
        out[name] = (out[name] * factor).astype(out[name].dtype)
    return out
```

```python
from contextlib import ExitStack

import concourse.bass as bass
from concourse import mybir

F32 = mybir.dt.float32
R32 = mybir.dt.float32r
I32 = mybir.dt.int32
ALU = mybir.AluOpType
ACT = mybir.ActivationFunctionType
AXX = mybir.AxisListType.X

P = 128
B, S, F = 8, 512, 512
H, D = 8, 64
HID = 1408
KT = F // P
ST = S // P
PAIRS = H // 2
MT = HID // P
ZERO_POINT = 128.0
EPS = 1e-5
QSCALE = 8.0 ** -0.5
SA, CA, GA, SB, CB, GB = range(6)

UNITS = MT + 3

RING0 = KT + ST
RING = H * ST + KT + ST + ST


def turn_pos(h, j, more=True):
    if h < 4 or not more:
        return ST * h + j
    if h == 4:
        return 16 + 2 * j
    return 24 + ST * (h - 5) + j


def norm_pos(f):
    return 17 + 2 * f


def v_pos(t):
    return 36 + t


def out_pos(s, more=True):
    return (40 if more else H * ST) + s


def filler_of(h):
    if h < 4:
        return 0, 2 + h // 2, h % 2
    return 1, (h - 4) // 2, h % 2


def adaln_block(nc, x, c_t, wmod, w_q, w_k, w_v, w_o, b_q, b_k, b_v, b_o, w_gate, w_up, w_down,
                s_gate, s_up, s_down, out):
    x1_dram = nc.dram_tensor("x1_scratch", [B, S, F], F32, kind="Internal").ap()
    gates_dram = nc.dram_tensor("gates_scratch", [2, B, F], F32, kind="Internal").ap()

    def tokens(a, b):
        return a[b, :, :].rearrange("(t p) f -> p t f", p=P)

    ctx = ExitStack()
    with ctx:
        at = [0]

        def sb(name, shape, dt=F32):
            n = 4
            for d in shape[1:]:
                n *= d
            t = nc.alloc_sbuf_tensor_at(name, shape, dt, offset=at[0])
            at[0] += (n + 31) // 32 * 32
            assert at[0] <= TOP, (name, at[0], TOP)
            return t

        at[0] = (nc.sbuf_base + 31) // 32 * 32
        TOP = at[0] + nc.sbuf_bytes_remaining // 32 * 32 - 32

        def sem(name):
            return ctx.enter_context(nc.semaphore(name))

        ident = sb("ident", [P, P])
        modc = sb("modc", [P, 4, KT, B])
        neg_half = sb("neg_half", [P, ST])
        three_halves = sb("three_halves", [P, ST])
        eps_t = sb("eps_t", [P, ST])
        stats = sb("stats", [P, ST, 6])
        mv = sb("mv", [P, ST, 2])
        veps = sb("veps", [P, ST])
        rstd = sb("rstd", [P, ST])
        newt = sb("newt", [P, ST])
        h32 = sb("h32", [P, 2, S])
        xn = sb("xn", [P, ST, F])
        xr = sb("xr", [P, ST, F])
        hT_hi = sb("hT_hi", [P, KT, S], R32)
        hT_lo = sb("hT_lo", [P, KT, S], R32)
        gate_bc = sb("gate_bc", [P, F])
        t32 = sb("t32", [P, 2, F])
        both = at[0]
        bqkv = sb("bqkv", [P, 3, PAIRS])
        bv_h = sb("bv_h", [D, H])
        c_sb = sb("c_sb", [P, KT, B])
        c_th = sb("c_th", [P, KT, B])
        c_silu = sb("c_silu", [P, KT, B])
        negmax = sb("negmax", [P, 2, ST])
        ssum = sb("ssum", [P, 2, ST])
        rinv = sb("rinv", [P, 2, ST])
        bo_f = sb("bo_f", [1, F])
        bo_hi = sb("bo_hi", [1, F], R32)
        bo_lo = sb("bo_lo", [1, F], R32)
        ones_f = sb("ones_f", [1, P])
        ones_r = sb("ones_r", [1, P], R32)
        W_hi = sb("W_hi", [P, 4, KT, F], R32)
        W_lo = sb("W_lo", [P, 4, KT, F], R32)
        qs = sb("qs", [P, 2, 2, S], R32)
        kh = sb("kh", [P, 2, 2, S], R32)
        kl = sb("kl", [P, 2, S], R32)
        v_sb = sb("v_sb", [P, ST, H, 2, D], R32)
        pr = sb("pr", [P, 2, ST, S])
        pt_hi = sb("pt_hi", [P, ST, S], R32)
        pt_lo = sb("pt_lo", [P, ST, S], R32)
        c32 = sb("c32", [D, S])
        a32 = sb("a32", [P, 2, S])
        a_hi = sb("a_hi", [P, PAIRS, S], R32)
        a_lo = sb("a_lo", [P, PAIRS, S], R32)
        rows = a32
        g_tmp = t32
        g_rows = [c32[0:B, :], a32[0:B, 1, :]]
        at[0] = both
        wg_hi = sb("wg_hi", [P, MT, KT, P], R32)
        wg_lo = sb("wg_lo", [P, MT, KT, P], R32)
        wu_hi = sb("wu_hi", [P, MT, KT, P], R32)
        wu_lo = sb("wu_lo", [P, MT, KT, P], R32)
        wd_hi = sb("wd_hi", [P, MT, F], R32)
        wd_lo = sb("wd_lo", [P, MT, F], R32)
        w_raw = sb("w_raw", [P, 3, F], I32)
        lo_square = sb("lo_square", [P, F])
        lo_sums = sb("lo_sums", [P, 3 * MT])
        lo_sum = sb("lo_sum", [P, 1])
        lo_row = sb("lo_row", [1, P])
        lo_all = sb("lo_all", [1, 1])
        lo_flag = sb("lo_flag", [1, 1], I32)
        g_hi = sb("g_hi", [P, 2, S], R32)
        g_lo = sb("g_lo", [P, 2, S], R32)
        tanh_sb = sb("tanh_sb", [P, S])
        a_sb = sb("a_sb", [P, S])
        g32 = sb("g32", [P, S])
        sdown_bc = sb("sdown_bc", [P, F])
        sg_half = sb("sg_half", [P, MT])
        su_col = sb("su_col", [P, MT])
        sgu_half = sb("sgu_half", [P, MT])

        psum = nc.alloc_psum_tensor("banks", [P, 8, 512], F32)
        SC = [psum[:, i, :] for i in range(4)]
        TB = [psum[:, 4 + i, :] for i in range(2)]
        PVB = psum[:, 6, :]
        PJ = psum[:, 7, :]

        const_ready = sem("const_ready")
        small_loaded = sem("small_loaded")
        stage_loaded = [sem(f"stage_loaded{i}") for i in range(3)]
        silu_step = sem("silu_step")
        bias_ready = sem("bias_ready")
        mod_mm = sem("mod_mm")
        mod_row = sem("mod_row")
        mod_turned = sem("mod_turned")
        mod_col = sem("mod_col")
        gate_step = sem("gate_step")
        gate_rows = sem("gate_rows")
        gates_stored = sem("gates_stored")
        w_hi_done = sem("w_hi_done")
        w_lo_done = sem("w_lo_done")
        xn_loaded = sem("xn_loaded")
        xr_loaded = sem("xr_loaded")
        gate_loaded = sem("gate_loaded")
        bn_done = sem("bn_done")
        aggr_begun = sem("aggr_begun")
        aggr_done = sem("aggr_done")
        ln_step = sem("ln_step")
        rstd_done = sem("rstd_done")
        ln_done = sem("ln_done")
        ring_ready = sem("ring_ready")
        ring_free = sem("ring_free")
        pj_ready = sem("pj_ready")
        pj_hi = sem("pj_hi")
        pj_done = sem("pj_done")
        h32_done = sem("h32_done")
        h_hi = sem("h_hi")
        v_hi = sem("v_hi")
        s_ready = sem("s_ready")
        max_done = sem("max_done")
        exp_done = sem("exp_done")
        rinv_done = sem("rinv_done")
        p_done = sem("p_done")
        pt_hi_done = sem("pt_hi_done")
        pv_ready = sem("pv_ready")
        c_done = sem("c_done")
        pv_free = sem("pv_free")
        ahi_done = sem("ahi_done")
        a_done = sem("a_done")
        x_done = sem("x_done")
        x1_stored = sem("x1_stored")
        fs_loaded = sem("fs_loaded")
        fs_step = sem("fs_step")
        wraw_loaded = sem("wraw_loaded")
        whi_done = sem("whi_done")
        wlo_done = sem("wlo_done")
        squares_done = sem("squares_done")
        lo_summed = sem("lo_summed")
        lo_turned = sem("lo_turned")
        lo_known = sem("lo_known")
        fx_loaded = sem("fx_loaded")
        fr_loaded = sem("fr_loaded")
        fg_loaded = sem("fg_loaded")
        fbn_done = sem("fbn_done")
        faggr_done = sem("faggr_done")
        fln_step = sem("fln_step")
        frstd_done = sem("frstd_done")
        fln_done = sem("fln_done")
        unit_ready = sem("unit_ready")
        unit_free = sem("unit_free")
        fh_hi = sem("fh_hi")
        fh_done = sem("fh_done")
        tanh_done = sem("tanh_done")
        a_step = sem("a_step")
        ghi_done = sem("ghi_done")
        g_done = sem("g_done")
        d_done = sem("d_done")
        gs_done = sem("gs_done")
        y_done = sem("y_done")
        fx_done = sem("fx_done")
        stored = sem("stored")

        block = ctx.enter_context(nc.Block())

        def ring(b, pos):
            return b * RING + RING0 + pos + 1

        STAGES = [("mod", SA), ("mod", CA), ("w", 2), ("w", 0), ("w", 1), ("mod", GA), ("w", 3),
                  ("mod", SB), ("mod", CB), ("mod", GB)]
        stage_buf = [pr[:, 0, :, :], pr[:, 1, :, :], xr[:, :, :]]
        MODS = [i for i, s in enumerate(STAGES) if s[0] == "mod"]
        WS = [i for i, s in enumerate(STAGES) if s[0] == "w"]
        COLS = {SA: 0, CA: 1, SB: 2, CB: 3}

        @block.sync
        def _(sp):
            sp.dma_start(xn[:, :, :], tokens(x, 0)).then_inc(xn_loaded, 16)
            sp.dma_start(c_sb[:, :, :], c_t.rearrange("(k p) b -> p k b", p=P)).then_inc(small_loaded, 16)
            w_dram = [w_q, w_k, w_v, w_o]
            for i, (kind, n) in enumerate(STAGES):
                if i >= 3:
                    used = i - 3
                    if STAGES[used][0] == "mod":
                        sp.wait_ge(mod_mm, MODS.index(used) + 1)
                    else:
                        sp.wait_ge(w_lo_done, WS.index(used) + 1)
                src = w_dram[n] if kind == "w" else wmod[:, n * F:(n + 1) * F]
                sp.dma_start(stage_buf[i % 3], src.rearrange("(k p) n -> p k n", p=P))\
                    .then_inc(stage_loaded[i % 3], 16)
                if i == 2:
                    for j, bias in enumerate((b_q, b_k)):
                        sp.dma_start(bqkv[:, j, :], bias).then_inc(small_loaded, 16)
                    sp.dma_start(bv_h[:, :], b_v).then_inc(small_loaded, 16)
                    sp.dma_start(bo_f[:, :], b_o).then_inc(small_loaded, 16)
            for g in range(2):
                sp.wait_ge(gate_rows, g + 1)
                sp.dma_start(gates_dram[g, :, :], g_rows[g]).then_inc(gates_stored, 16)
            sp.wait_ge(gates_stored, 32)
            sp.wait_ge(mod_mm, len(MODS))
            sp.wait_ge(w_lo_done, len(WS))
            sp.dma_start(xr[:, :, :], tokens(x, 0)).then_inc(xr_loaded, 16)
            sp.dma_start(gate_bc[:, :], gates_dram[0, 0:1, :].partition_broadcast(P)).then_inc(gate_loaded, 16)

            def stores(b):
                for s in range(ST):
                    sp.wait_ge(x_done, b * ST + s + 3)
                    sp.dma_start(x1_dram[b, s * P:(s + 1) * P, :], xr[:, s, :]).then_inc(x1_stored, 16)

            with sp.Fori(0, B - 1) as b:
                sp.wait_ge(pj_ready, b * H + 1)
                sp.dma_start(xn[:, :, :], tokens(x, b + 1)).then_inc(xn_loaded, 16)
                stores(b)
                sp.wait_ge(x1_stored, b * 64 + 64)
                sp.dma_start(xr[:, :, :], tokens(x, b + 1)).then_inc(xr_loaded, 16)
                sp.dma_start(gate_bc[:, :], gates_dram[0, bass.ds(b + 1, 1), :].partition_broadcast(P))\
                    .then_inc(gate_loaded, 16)
            stores(B - 1)
            sp.wait_ge(x1_stored, B * 64)

            sp.dma_start(xn[:, :, :], tokens(x1_dram, 0)).then_inc(fx_loaded, 16)
            sp.dma_start(sg_half[:, :], s_gate).then_inc(fs_loaded, 16)
            sp.dma_start(su_col[:, :], s_up).then_inc(fs_loaded, 16)
            sp.dma_start(sdown_bc[:, :], s_down.partition_broadcast(P)).then_inc(fs_loaded, 16)
            sp.dma_start(xr[:, :, :], tokens(x1_dram, 0)).then_inc(fr_loaded, 16)
            sp.dma_start(gate_bc[:, :], gates_dram[1, 0:1, :].partition_broadcast(P)).then_inc(fg_loaded, 16)

            def next_xn(b):
                sp.wait_ge(unit_ready, b * UNITS + 3)
                sp.dma_start(xn[:, :, :], tokens(x1_dram, b + 1)).then_inc(fx_loaded, 16)

            for m in range(MT):
                if m:
                    sp.wait_ge(wlo_done, m)
                for j, w in enumerate((w_gate, w_up, w_down)):
                    sp.dma_start(w_raw[:, j, :], w[m, :, :]).then_inc(wraw_loaded, 16)
                if m == 2:
                    next_xn(0)
            sp.wait_ge(lo_summed, 1)
            sp.dma_start(lo_row[0:1, :], lo_sum[:, :]).then_inc(lo_turned, 16)

            def out_stores(b):
                for s in range(ST):
                    sp.wait_ge(fx_done, b * ST + s + 3)
                    sp.dma_start(out[b, s * P:(s + 1) * P, :], xr[:, s, :]).then_inc(stored, 16)

            def turn_over(b):
                out_stores(b)
                sp.wait_ge(stored, b * 64 + 64)
                sp.dma_start(xr[:, :, :], tokens(x1_dram, b + 1)).then_inc(fr_loaded, 16)
                sp.dma_start(gate_bc[:, :], gates_dram[1, bass.ds(b + 1, 1), :].partition_broadcast(P))\
                    .then_inc(fg_loaded, 16)

            turn_over(0)
            with sp.Fori(1, B - 1) as b:
                next_xn(b)
                turn_over(b)
            out_stores(B - 1)
            sp.wait_ge(stored, B * 64)

        @block.tensor
        def _(pe):
            def turn_norm(f, bank):
                for t in range(ST):
                    mm = pe.transpose(bank[:, t * P:(t + 1) * P], xn[:, t, f * P:(f + 1) * P], ident[:, :])
                return mm

            def project(bank, w, m, steps=range(12), ready=None):
                for i in steps:
                    k, part = divmod(i, 3)
                    if part == 0 and ready is not None:
                        ready(k)
                    lhs = (W_lo if part == 2 else W_hi)[:, w, k, m * P:(m + 1) * P]
                    rhs = (hT_lo if part == 1 else hT_hi)[:, k, :]
                    mm = pe.matmul(bank, lhs, rhs, start=(i == 0), stop=(i == 11))
                return mm

            def scores(b, h, first=False):
                pb, w = h // 2 % 2, h % 2
                pe.wait_ge(pj_done, b * H + 2 * (h // 2) + 2)
                lo = slice(0, D) if w == 0 else slice(D, P)
                for st in range(ST):
                    if not first:
                        pe.wait_ge(exp_done, b * 32 + 4 * h + st - 3)
                    cols = slice(st * P, (st + 1) * P)
                    pe.matmul(SC[st], qs[:, pb, w, cols], kh[:, pb, w, :], start=True, stop=False)
                    pe.matmul(SC[st], qs[lo, pb, w, cols], kl[lo, pb, :], start=False, stop=True)\
                        .then_inc(s_ready, 1)

            def turn(b, h, j, more):
                n = turn_pos(h, j, more)
                pe.wait_ge(ring_free, ring(b, n) - 2)
                if j == 0:
                    pe.wait_ge(p_done, b * 32 + 4 * h + 4)
                for st in range(ST):
                    mm = pe.transpose(TB[n % 2][:, st * P:(st + 1) * P],
                                      pr[:, h % 2, st, j * P:(j + 1) * P], ident[:, :])
                mm.then_inc(ring_ready, 1)

            def pv(b, h, j, more):
                if j == 0:
                    pe.wait_ge(pv_free, b * H + h + 1)
                pe.wait_ge(ring_free, ring(b, turn_pos(h, j, more)))
                lhs = v_sb[:, j, h, :, :].rearrange("p a d -> p (a d)")
                pe.matmul(PVB, lhs, pt_hi[:, j, :], start=(j == 0), stop=False)
                mm = pe.matmul(PVB, lhs, pt_lo[:, j, :], start=False, stop=(j == ST - 1))
                if j == ST - 1:
                    mm.then_inc(pv_ready, 1)

            def values(t, bank):
                for i in range(12):
                    k, part = divmod(i, 3)
                    lhs = (hT_lo if part == 1 else hT_hi)[:, k, t * P:(t + 1) * P]
                    rhs = (W_lo if part == 2 else W_hi)[:, 2, k, :]
                    mm = pe.matmul(bank, lhs, rhs, start=(i == 0), stop=(i == 11))
                return mm

            def output(s, bank):
                pe.matmul(bank, ones_r[:, :], bo_hi[:, :], start=True, stop=False)
                pe.matmul(bank, ones_r[:, :], bo_lo[:, :], start=False, stop=False)
                for i in range(12):
                    k, part = divmod(i, 3)
                    lhs = (a_lo if part == 1 else a_hi)[:, k, s * P:(s + 1) * P]
                    rhs = (W_lo if part == 2 else W_hi)[:, 3, k, :]
                    mm = pe.matmul(bank, lhs, rhs, start=False, stop=(i == 11))
                return mm

            pe.wait_ge(silu_step, 3)
            pe.wait_ge(const_ready, 1)

            def mod_rows(n):
                i = MODS[n]
                pe.wait_ge(stage_loaded[i % 3], 16 * (i // 3 + 1))
                if n >= 2:
                    pe.wait_ge(mod_row, n - 1)
                for k in range(KT):
                    mm = pe.matmul(SC[n % 2][0:B, :], c_silu[:, k, :], stage_buf[i % 3][:, k, :],
                                   start=(k == 0), stop=(k == KT - 1))
                mm.then_inc(mod_mm, 1)

            def mod_turn(n):
                pe.wait_ge(mod_row, n + 1)
                for f in range(KT):
                    mm = pe.transpose(SC[2 + n % 2][:, f * B:(f + 1) * B],
                                      rows[0:B, n % 2, f * P:(f + 1) * P], ident[0:B, 0:B])
                mm.then_inc(mod_turned, 1)

            def modulation(n):
                mod_rows(n)
                if STAGES[MODS[n]][1] in COLS:
                    mod_turn(n)

            for n in range(2):
                modulation(n)
            for f in range(KT):
                if f == 0:
                    pe.wait_ge(ln_done, ST)
                if f >= 2:
                    pe.wait_ge(ring_free, f - 1)
                turn_norm(f, TB[f % 2]).then_inc(ring_ready, 1)
            for n in range(2, len(MODS)):
                modulation(n)
            pe.wait_ge(w_lo_done, len(WS))
            for i in range(4):
                if i:
                    pe.wait_ge(pj_done, i)
                project(PJ, i % 2, i // 2, ready=lambda k: pe.wait_ge(ring_free, k + 1)).then_inc(pj_ready, 1)
                if i == 1:
                    scores(0, 0, first=True)
            for t in range(ST):
                pe.wait_ge(ring_free, KT + t - 1)
                values(t, TB[t % 2]).then_inc(ring_ready, 1)

            def filler(b, h, steps):
                nxt, pair, qk = filler_of(h)
                bb = b + nxt
                use = bb * H + 2 * pair + qk
                if steps[0] == 0:
                    pe.wait_ge(pj_done, use)
                mm = project(PJ, qk, pair, steps,
                             ready=(lambda k: pe.wait_ge(ring_free, ring(b, norm_pos(k)))) if h == 4 else None)
                if steps[-1] == 11:
                    mm.then_inc(pj_ready, 1)

            def attention(b, more):
                for h in range(H):
                    fill = h < 4 or more
                    if h < H - 1:
                        scores(b, h + 1)
                    elif more:
                        scores(b + 1, 0)
                    if fill and h != 4:
                        filler(b, h, range(0, 4))
                    if h:
                        pv(b, h - 1, 2, more)
                        pv(b, h - 1, 3, more)

                    def norm_turn(f):
                        if h == 4 and more:
                            if f == 0:
                                pe.wait_ge(ln_done, b * ST + 2 * ST)
                            pe.wait_ge(ring_free, ring(b, norm_pos(f)) - 2)
                            turn_norm(f, TB[norm_pos(f) % 2]).then_inc(ring_ready, 1)

                    turn(b, h, 0, more)
                    norm_turn(0)
                    if fill and h != 4:
                        filler(b, h, range(4, 8))
                    turn(b, h, 1, more)
                    norm_turn(1)
                    if fill and h != 4:
                        filler(b, h, range(8, 12))
                    turn(b, h, 2, more)
                    pv(b, h, 0, more)
                    norm_turn(2)
                    turn(b, h, 3, more)
                    pv(b, h, 1, more)
                    norm_turn(3)
                    if h == 4 and fill:
                        filler(b, h, range(0, 12))
                pv(b, H - 1, 2, more)
                pv(b, H - 1, 3, more)
                for t in range(ST if more else 0):
                    pe.wait_ge(ring_free, ring(b, v_pos(t)) - 2)
                    values(t, TB[v_pos(t) % 2]).then_inc(ring_ready, 1)
                for s in range(ST):
                    n = out_pos(s, more)
                    pe.wait_ge(ring_free, ring(b, n) - 2)
                    if s == 0:
                        pe.wait_ge(a_done, b * PAIRS + PAIRS)
                    output(s, TB[n % 2]).then_inc(ring_ready, 1)

            with pe.Fori(0, B - 1) as b:
                attention(b, True)
            attention(B - 1, False)

            G = [psum[:, 0, :], psum[:, 2, :]]
            U = [psum[:, 1, :], psum[:, 3, :]]
            Y = [psum[:, 4 + s, :] for s in range(ST)]
            NORM_UNITS = [(0, 1), (2,), (3,)]

            def ff_norm(n0, u, first):
                fs = NORM_UNITS[u]
                if not first or u == 2:
                    pe.wait_ge(unit_free, n0 + u - 1)
                for f in fs:
                    bank = (G if f in (0, 2, 3) else U)[u % 2]
                    for t in range(ST):
                        mm = pe.transpose(bank[:, t * P:(t + 1) * P], xn[:, t, f * P:(f + 1) * P], ident[:, :])
                mm.then_inc(unit_ready, 1)

            def gate_up(b, m, bi, parts):
                u = (3 + m) % 2
                pe.wait_ge(unit_free, b * UNITS + 3 + m - 1)
                if bi == 0:
                    pe.wait_ge(wlo_done, m + 1)
                for w_hi_, w_lo_, bank in ((wg_hi, wg_lo, G[u]), (wu_hi, wu_lo, U[u])):
                    for i in range(KT * parts):
                        k, part = divmod(i, parts)
                        if m == 0 and part == 0 and bank is G[u]:
                            pe.wait_ge(fh_done, b * KT + k + 1)
                        mm = pe.matmul(bank, (w_lo_ if part == 2 else w_hi_)[:, m, k, :],
                                       (hT_lo if part == 1 else hT_hi)[:, k, :],
                                       start=(i == 0), stop=(i == KT * parts - 1))
                mm.then_inc(unit_ready, 1)

            def down(b, m, parts):
                pe.wait_ge(g_done, b * MT + m + 1)
                for s in range(ST):
                    if m == 0:
                        pe.wait_ge(y_done, b * ST + s + 1)
                    cols = slice(s * P, (s + 1) * P)
                    pe.matmul(Y[s], g_hi[:, m % 2, cols], wd_hi[:, m, :], start=(m == 0), stop=False)
                    last = m == MT - 1
                    mm = pe.matmul(Y[s], g_lo[:, m % 2, cols], wd_hi[:, m, :], start=False,
                                   stop=last and parts == 2)
                    if parts == 3:
                        mm = pe.matmul(Y[s], g_hi[:, m % 2, cols], wd_lo[:, m, :], start=False, stop=last)
                mm.then_inc(d_done, 1)

            def feed_forward(b, bi, more, parts):
                for m in range(MT):
                    gate_up(b, m, bi, parts)
                    if m:
                        down(b, m - 1, parts)
                if more:
                    pe.wait_ge(fln_done, b * ST + 2 * ST)
                    for u in range(3):
                        ff_norm(b * UNITS + UNITS, u, False)
                down(b, MT - 1, parts)

            pe.wait_ge(fln_done, ST)
            for u in range(3):
                ff_norm(0, u, True)
            feed_forward(0, 0, True, 3)

            def other_batches(parts):
                with pe.Fori(1, B - 1) as b:
                    feed_forward(b, 1, True, parts)
                feed_forward(B - 1, B - 1, False, parts)

            pe.wait_ge(lo_known, 1)
            with pe.If(pe.value_load(lo_flag[0:1, 0:1]) != 0):
                other_batches(3)
            with pe.Else():
                other_batches(2)
            pe.end_ifs()

        @block.scalar
        def _(act):
            act.wait_ge(small_loaded, 16 * 5)
            act.activation(c_th[:, :, :], c_sb[:, :, :], ACT.Tanh, scale=0.5).then_inc(silu_step, 1)
            act.mul(bqkv[:, 0, :], bqkv[:, 0, :], QSCALE).then_inc(bias_ready, 1)
            act.activation(bo_hi[:, :], bo_f[:, :], ACT.Copy).then_inc(bias_ready, 1)

            def split_hi(n):
                i = WS[n]
                w = STAGES[i][1]
                act.wait_ge(stage_loaded[i % 3], 16 * (i // 3 + 1))
                act.activation(W_hi[:, w, :, :], stage_buf[i % 3], ACT.Copy,
                               scale=QSCALE if w == 0 else 1.0).then_inc(w_hi_done, 1)

            def norm_hi(b, f):
                act.wait_ge(h32_done, b * KT + f + 1)
                act.activation(hT_hi[:, f, :], h32[:, f % 2, :], ACT.Copy).then_inc(h_hi, 1)

            def proj_hi(b, pair, qk):
                pb = pair % 2
                act.wait_ge(pj_ready, b * H + 2 * pair + qk + 1)
                halves = ((0, slice(0, D)), (1, slice(D, P)))
                for w, src in halves:
                    for dst in ((src,) if qk == 0 else (slice(0, D), slice(D, P))):
                        a = act.activation((qs if qk == 0 else kh)[dst, pb, w, :], PJ[src, :], ACT.Identity,
                                           bias=bqkv[src, qk, pair:pair + 1], scale=1.0)
                a.then_inc(pj_hi, 1)

            def exps(b, h, st):
                act.wait_ge(max_done, b * 32 + 4 * h + st + 1)
                act.activation(pr[:, h % 2, st, :], SC[st], ACT.Exp, bias=negmax[:, h % 2, st:st + 1],
                               scale=1.0, accum_out=ssum[:, h % 2, st:st + 1]).then_inc(exp_done, 1)

            def weights_hi(b, h, j, more):
                n = turn_pos(h, j, more)
                act.wait_ge(ring_ready, ring(b, n))
                act.activation(pt_hi[:, j, :], TB[n % 2], ACT.Copy).then_inc(pt_hi_done, 1)

            def lower_half(b, h):
                act.wait_ge(pv_ready, b * H + h + 1)
                act.activation(c32[:, :], PVB[D:P, :], ACT.Copy).then_inc(c_done, 1)

            def v_his(b, t, uses, bank):
                act.wait_ge(ring_ready, uses)
                act.activation(v_sb[:, t, :, 0, :], bank.rearrange("p (h d) -> p h d", d=D), ACT.Copy)\
                    .then_inc(v_hi, 1)

            split_hi(0)
            for f in range(KT):
                norm_hi(0, f)
            for n in range(1, len(WS)):
                split_hi(n)
            act.wait_ge(bias_ready, 4)
            for pair, qk in ((0, 0), (0, 1)):
                proj_hi(0, pair, qk)
            for st in range(ST):
                exps(0, 0, st)
            for pair, qk in ((1, 0), (1, 1)):
                proj_hi(0, pair, qk)
            for t in range(ST):
                v_his(0, t, KT + t + 1, TB[t % 2])

            act.wait_ge(gates_stored, 32)
            def attention(b, more):
                for h in range(H):
                    if h and h != 5:
                        weights_hi(b, h - 1, 3, more)
                    if h < H - 1 or more:
                        nb, nh = (b, h + 1) if h < H - 1 else (b + 1, 0)
                        for st in range(ST):
                            exps(nb, nh, st)
                    if h:
                        lower_half(b, h - 1)
                    for j in range(3):
                        weights_hi(b, h, j, more)
                        if h == 4 and more:
                            norm_hi(b + 1, j)
                    if h == 4:
                        weights_hi(b, h, 3, more)
                        if more:
                            norm_hi(b + 1, 3)
                    if h < 4 or more:
                        nxt, pair, qk = filler_of(h)
                        proj_hi(b + nxt, pair, qk)
                weights_hi(b, H - 1, 3, more)
                lower_half(b, H - 1)
                if more:
                    for t in range(ST):
                        v_his(b + 1, t, ring(b, v_pos(t)), TB[v_pos(t) % 2])

            with act.Fori(0, B - 1) as b:
                attention(b, True)
            attention(B - 1, False)

            def weights_split(m):
                act.wait_ge(wraw_loaded, 48 * (m + 1))
                for j, w in enumerate((wg_hi[:, m, :, :].rearrange("p k n -> p (k n)"),
                                       wu_hi[:, m, :, :].rearrange("p k n -> p (k n)"), wd_hi[:, m, :])):
                    a = act.activation(w, w_raw[:, j, :], ACT.Copy, bias=-ZERO_POINT)
                a.then_inc(whi_done, 1)

            def squares(m):
                act.wait_ge(wlo_done, m + 1)
                for j, w in enumerate((wg_lo[:, m, :, :].rearrange("p k n -> p (k n)"),
                                       wu_lo[:, m, :, :].rearrange("p k n -> p (k n)"), wd_lo[:, m, :])):
                    if m or j:
                        act.wait_ge(squares_done, 3 * m + j)
                    act.activation(lo_square[:, :], w.bitcast(F32), ACT.Square,
                                   accum_out=lo_sums[:, 3 * m + j:3 * m + j + 1]).then_inc(squares_done, 1)

            def ff_norm_hi(b, f):
                act.wait_ge(unit_free, b * UNITS + (1, 1, 2, 3)[f])
                act.activation(hT_hi[:, f, :], h32[:, f % 2, :], ACT.Copy).then_inc(fh_hi, 1)

            G = [psum[:, 0, :], psum[:, 2, :]]
            act.wait_ge(fs_step, 2)
            weights_split(0)
            for f in range(KT):
                ff_norm_hi(0, f)

            def feed_forward(b, bi, more):
                for m in range(MT):
                    if bi == 0 and m + 1 < MT:
                        weights_split(m + 1)
                    act.wait_ge(unit_ready, b * UNITS + 3 + m + 1)
                    act.activation(tanh_sb[:, :], G[(3 + m) % 2], ACT.Tanh, scale=sg_half[:, m:m + 1])\
                        .then_inc(tanh_done, 1)
                    act.wait_ge(unit_free, b * UNITS + 3 + m + 1)
                    if bi or m >= 2:
                        act.wait_ge(d_done, b * MT + max(m - 1, 0))
                    act.activation(g_hi[:, m % 2, :], g32[:, :], ACT.Copy).then_inc(ghi_done, 1)
                    if bi == 0:
                        squares(m)
                if more:
                    for f in range(KT):
                        ff_norm_hi(b + 1, f)

            feed_forward(0, 0, True)
            with act.Fori(1, B - 1) as b:
                feed_forward(b, 1, True)
            feed_forward(B - 1, B - 1, False)


        @block.vector
        def _(dve):
            def norm_stats(b, loaded, bn, aggr, done):
                dve.wait_ge(loaded, b * 16 + 16)
                for t in range(ST):
                    dve.bn_stats(stats[:, t, :], xn[:, t, :]).then_inc(bn, 1)
                dve.wait_ge(bn, b * ST + ST)
                dve.sem_inc(aggr_begun, 1)
                for t in range(ST):
                    dve.bn_aggr(mv[:, t, :], stats[:, t, :]).then_inc(aggr, 1)

            def norm_scale(b, rstd_sem, done):
                dve.wait_ge(rstd_sem, b + 1)
                for t in range(ST):
                    dve.tensor_scalar(xn[:, t, :], xn[:, t, :], mv[:, t, 0:1], rstd[:, t:t + 1],
                                      ALU.subtract, ALU.mult).then_inc(done, 1)

            def modulate(f, b, kind, bank):
                return dve.tensor_scalar(h32[:, f % 2, :], bank, modc[:, kind + 1, f, bass.ds(b, 1)],
                                         modc[:, kind, f, bass.ds(b, 1)], ALU.mult, ALU.add)

            def norm_lo(f):
                return dve.tensor_tensor(hT_lo[:, f, :], h32[:, f % 2, :], hT_hi[:, f, :].bitcast(F32),
                                         ALU.subtract)

            def norm_part(b, f, uses, bank):
                dve.wait_ge(ring_ready, uses)
                modulate(f, b, 0, bank).then_inc(h32_done, 1)
                dve.wait_ge(h_hi, b * KT + f + 1)
                norm_lo(f).then_inc(ring_free, 1)

            dve.wait_ge(silu_step, 1)
            dve.scalar_tensor_tensor(c_silu[:, :, :], c_th[:, :, :], 1.0, c_sb[:, :, :], ALU.add, ALU.mult)\
                .then_inc(silu_step, 1)
            dve.wait_ge(silu_step, 2)
            dve.tensor_scalar(c_silu[:, :, :], c_silu[:, :, :], 0.5, None, ALU.mult).then_inc(silu_step, 1)
            norm_stats(0, xn_loaded, bn_done, aggr_done, ln_done)
            norm_scale(0, rstd_done, ln_done)
            dve.wait_ge(bias_ready, 2)
            dve.tensor_tensor(bo_lo[:, :], bo_f[:, :], bo_hi[:, :].bitcast(F32), ALU.subtract).then_inc(bias_ready, 1)
            dve.tensor_copy(ones_r[:, :], ones_f[:, :]).then_inc(bias_ready, 1)

            def modulation(n):
                kind = STAGES[MODS[n]][1]
                bank = SC[n % 2][0:B, :]
                dve.wait_ge(mod_mm, n + 1)
                if kind in COLS:
                    dve.tensor_copy(rows[0:B, n % 2, :], bank).then_inc(mod_row, 1)
                    col = COLS[kind]
                    dve.wait_ge(mod_turned, col + 1)
                    turned = SC[2 + n % 2][:, 0:KT * B].rearrange("p (k b) -> p k b", b=B)
                    dve.tensor_scalar(modc[:, col, :, :], turned, float(kind in (CA, CB)), None, ALU.add)\
                        .then_inc(mod_col, 1)
                else:
                    g = int(kind == GB)
                    dve.tensor_scalar(g_tmp[0:B, 0, :], bank, 0.0, 2.0, ALU.is_ge, ALU.mult).then_inc(gate_step, 1)
                    dve.tensor_scalar(g_tmp[0:B, 1, :], bank, -1.0, 0.25, ALU.mult, ALU.max).then_inc(gate_step, 1)
                    dve.wait_ge(gate_step, 2 * g + 2)
                    dve.tensor_tensor(g_tmp[0:B, 1, :], bank, g_tmp[0:B, 1, :], ALU.max).then_inc(mod_row, 1)
                    dve.wait_ge(mod_row, n + 1)
                    dve.scalar_tensor_tensor(g_rows[g], g_tmp[0:B, 0, :], -1.0, g_tmp[0:B, 1, :],
                                             ALU.add, ALU.mult).then_inc(gate_rows, 1)

            def split_lo(n):
                i = WS[n]
                w = STAGES[i][1]
                dve.wait_ge(w_hi_done, n + 1)
                dve.scalar_tensor_tensor(W_lo[:, w, :, :].rearrange("p k n -> p (k n)"),
                                         stage_buf[i % 3].rearrange("p k n -> p (k n)"),
                                         QSCALE if w == 0 else 1.0,
                                         W_hi[:, w, :, :].bitcast(F32).rearrange("p k n -> p (k n)"),
                                         ALU.mult, ALU.subtract).then_inc(w_lo_done, 1)

            modulation(0)
            modulation(1)
            split_lo(0)
            dve.wait_ge(mod_col, 2)
            for f in range(KT):
                norm_part(0, f, f + 1, TB[f % 2])
            for i, (kind, n) in enumerate(STAGES[3:], 3):
                if kind == "w":
                    split_lo(WS.index(i))
                else:
                    modulation(MODS.index(i))

            def proj_lo(b, pair, qk):
                pb = pair % 2
                dve.wait_ge(pj_hi, b * H + 2 * pair + qk + 1)
                lo_dst = [(slice(D, P) if qk == 0 else slice(0, D)), (slice(0, D) if qk == 0 else slice(D, P))]
                for w, src in ((0, slice(0, D)), (1, slice(D, P))):
                    hi = (qs if qk == 0 else kh)[src, pb, w, :].bitcast(F32)
                    dst = qs[lo_dst[w], pb, w, :] if qk == 0 else kl[lo_dst[w], pb, :]
                    d = dve.scalar_tensor_tensor(dst, PJ[src, :], bqkv[src, qk, pair:pair + 1], hi,
                                                 ALU.add, ALU.subtract)
                d.then_inc(pj_done, 1)

            def row_max(b, h, st):
                dve.wait_ge(s_ready, b * 32 + 4 * h + st + 1)
                dve.tensor_reduce(negmax[:, h % 2, st:st + 1], SC[st], AXX, ALU.max, negate=True)\
                    .then_inc(max_done, 1)

            def row_recip(b, h, st):
                dve.wait_ge(exp_done, b * 32 + 4 * h + st + 1)
                dve.reciprocal(rinv[:, h % 2, st:st + 1], ssum[:, h % 2, st:st + 1]).then_inc(rinv_done, 1)

            def softmax_rows(b, h):
                row_max(b, h, 0)
                row_max(b, h, 1)
                row_recip(b, h, 0)
                row_max(b, h, 2)
                row_recip(b, h, 1)
                row_max(b, h, 3)
                row_recip(b, h, 2)
                row_recip(b, h, 3)

            def weights_lo(b, h, j, more):
                dve.wait_ge(pt_hi_done, b * 32 + 4 * h + j + 1)
                dve.tensor_tensor(pt_lo[:, j, :], TB[turn_pos(h, j, more) % 2], pt_hi[:, j, :].bitcast(F32),
                                  ALU.subtract).then_inc(ring_free, 1)

            def join_halves(b, h):
                dve.wait_ge(c_done, b * H + h + 1)
                rows_ = slice(D * (h % 2), D * (h % 2) + D)
                dve.scalar_tensor_tensor(a32[rows_, h // 2 % 2, :], PVB[0:D, :], bv_h[:, h:h + 1], c32[:, :],
                                         ALU.add, ALU.add).then_inc(pv_free, 1)

            def result_hi(b, pair):
                dve.wait_ge(pv_free, b * H + 2 * pair + 3)
                dve.tensor_copy(a_hi[:, pair, :], a32[:, pair % 2, :]).then_inc(ahi_done, 1)

            def v_los(b, t, bank):
                dve.wait_ge(v_hi, b * ST + t + 1)
                dve.tensor_tensor(v_sb[:, t, :, 1, :], bank.rearrange("p (h d) -> p h d", d=D),
                                  v_sb[:, t, :, 0, :].bitcast(F32), ALU.subtract).then_inc(ring_free, 1)

            dve.sem_inc(pv_free, 1)
            dve.sem_inc(y_done, ST)
            proj_lo(0, 0, 0)
            proj_lo(0, 0, 1)
            softmax_rows(0, 0)
            proj_lo(0, 1, 0)
            proj_lo(0, 1, 1)
            for t in range(ST):
                v_los(0, t, TB[t % 2])

            def attention(b, more):
                for h in range(H):
                    if h and h != 5:
                        weights_lo(b, h - 1, 3, more)
                    if h < H - 1:
                        softmax_rows(b, h + 1)
                    elif more:
                        softmax_rows(b + 1, 0)
                    if h:
                        join_halves(b, h - 1)
                        if h % 2 == 0:
                            result_hi(b, h // 2 - 1)
                    if h == 1 and more:
                        norm_stats(b + 1, xn_loaded, bn_done, aggr_done, ln_done)
                    if h == 3 and more:
                        norm_scale(b + 1, rstd_done, ln_done)
                    for j in range(4 if h == 4 else 3):
                        weights_lo(b, h, j, more)
                        if h == 4 and more:
                            norm_part(b + 1, j, ring(b, norm_pos(j)), TB[norm_pos(j) % 2])
                    if h < 4 or more:
                        nxt, pair, qk = filler_of(h)
                        proj_lo(b + nxt, pair, qk)
                weights_lo(b, H - 1, 3, more)
                join_halves(b, H - 1)
                result_hi(b, PAIRS - 1)
                if more:
                    for t in range(ST):
                        v_los(b + 1, t, TB[v_pos(t) % 2])
                dve.wait_ge(gate_loaded, b * 16 + 16)
                for s in range(ST):
                    n = out_pos(s, more)
                    dve.wait_ge(ring_ready, ring(b, n))
                    dve.wait_ge(x_done, b * ST + s + 1)
                    dve.tensor_tensor(t32[:, s % 2, :], TB[n % 2], gate_bc[:, :], ALU.mult).then_inc(ring_free, 1)

            with dve.Fori(0, B - 1) as b:
                attention(b, True)
            attention(B - 1, False)

            G = [psum[:, 0, :], psum[:, 2, :]]
            U = [psum[:, 1, :], psum[:, 3, :]]
            Y = [psum[:, 4 + s, :] for s in range(ST)]

            def split_lo_b(m):
                dve.wait_ge(whi_done, m + 1)
                for j, (lo, hi) in enumerate(((wg_lo, wg_hi), (wu_lo, wu_hi))):
                    dve.scalar_tensor_tensor(lo[:, m, :, :].rearrange("p k n -> p (k n)"), w_raw[:, j, :], -ZERO_POINT,
                                             hi[:, m, :, :].bitcast(F32).rearrange("p k n -> p (k n)"),
                                             ALU.add, ALU.subtract)
                dve.scalar_tensor_tensor(wd_lo[:, m, :], w_raw[:, 2, :], -ZERO_POINT, wd_hi[:, m, :].bitcast(F32),
                                         ALU.add, ALU.subtract).then_inc(wlo_done, 1)

            def ff_norm_part(b):
                for u, fs in enumerate(((0, 1), (2,), (3,))):
                    dve.wait_ge(unit_ready, b * UNITS + u + 1)
                    if u:
                        dve.wait_ge(fh_done, b * KT + u)
                    for f in fs:
                        d = modulate(f, b, 2, (G if f != 1 else U)[u % 2])
                    d.then_inc(unit_free, 1)
                    for f in fs:
                        dve.wait_ge(fh_hi, b * KT + f + 1)
                        norm_lo(f).then_inc(fh_done, 1)

            def weights_flag():
                dve.wait_ge(squares_done, 3 * MT)
                dve.tensor_reduce(lo_sum[:, :], lo_sums[:, :], AXX, ALU.max).then_inc(lo_summed, 1)
                dve.wait_ge(lo_turned, 16)
                dve.tensor_reduce(lo_all[:, :], lo_row[:, :], AXX, ALU.max).then_inc(lo_summed, 1)
                dve.wait_ge(lo_summed, 2)
                dve.tensor_scalar(lo_flag[:, :], lo_all[:, :], 0.0, None, ALU.is_gt).then_inc(lo_known, 1)

            norm_stats(0, fx_loaded, fbn_done, faggr_done, fln_done)
            norm_scale(0, frstd_done, fln_done)
            dve.wait_ge(fs_loaded, 48)
            dve.scalar_tensor_tensor(sgu_half[:, :], sg_half[:, :], 0.5, su_col[:, :], ALU.mult, ALU.mult)\
                .then_inc(fs_step, 1)
            dve.wait_ge(fs_step, 1)
            dve.tensor_scalar(sg_half[:, :], sg_half[:, :], 0.5, None, ALU.mult).then_inc(fs_step, 1)
            split_lo_b(0)
            dve.wait_ge(mod_col, 4)
            ff_norm_part(0)

            def feed_forward(b, bi, more):
                for m in range(MT):
                    if bi == 0 and m + 1 < MT:
                        split_lo_b(m + 1)
                    u = (3 + m) % 2
                    dve.wait_ge(tanh_done, b * MT + m + 1)
                    dve.scalar_tensor_tensor(a_sb[:, :], tanh_sb[:, :], 1.0, G[u], ALU.add, ALU.mult)\
                        .then_inc(a_step, 1)
                    dve.wait_ge(a_step, b * MT + m + 1)
                    dve.scalar_tensor_tensor(g32[:, :], U[u], sgu_half[:, m:m + 1], a_sb[:, :],
                                             ALU.mult, ALU.mult).then_inc(unit_free, 1)
                    dve.wait_ge(ghi_done, b * MT + m + 1)
                    dve.tensor_tensor(g_lo[:, m % 2, :], g32[:, :], g_hi[:, m % 2, :].bitcast(F32),
                                      ALU.subtract).then_inc(g_done, 1)
                    if m == 2 and more:
                        norm_stats(b + 1, fx_loaded, fbn_done, faggr_done, fln_done)
                    if m == 5 and more:
                        norm_scale(b + 1, frstd_done, fln_done)
                    if bi == 0 and m == MT - 1:
                        weights_flag()
                if more:
                    ff_norm_part(b + 1)
                dve.wait_ge(gs_done, b + 1)
                dve.wait_ge(d_done, b * MT + MT)
                for s in range(ST):
                    dve.wait_ge(fx_done, b * ST + s + 1)
                    dve.tensor_tensor(t32[:, s % 2, :], Y[s], gate_bc[:, :], ALU.mult).then_inc(y_done, 1)

            feed_forward(0, 0, True)
            with dve.Fori(1, B - 1) as b:
                feed_forward(b, 1, True)
            feed_forward(B - 1, B - 1, False)

        @block.gpsimd
        def _(pool):
            pool.memset(ident[:, :], 0.0).then_inc(ln_step, 1)
            pool.memset(neg_half[:, :], -0.5).then_inc(ln_step, 1)
            pool.memset(ones_f[:, :], 1.0).then_inc(ln_step, 1)
            pool.memset(eps_t[:, :], EPS).then_inc(ln_step, 1)
            pool.memset(three_halves[:, :], 1.5).then_inc(ln_step, 1)
            pool.wait_ge(ln_step, 5)
            pool.affine_select(out=ident[:, :], in_=ident[:, :], compare_op=ALU.not_equal, fill=1.0, base=0,
                               pattern=[[-1, P]], channel_multiplier=1).then_inc(const_ready, 1)
            pool.sem_inc(x_done, 2)
            pool.sem_inc(fx_done, 2)

            def inv_std(b, aggr, step, base, done):
                def after(k):
                    pool.wait_ge(step, b * 6 + base + k)

                pool.wait_ge(aggr, b * ST + ST)
                pool.tensor_tensor(veps[:, :], mv[:, :, 1], eps_t[:, :], ALU.add).then_inc(step, 1)
                after(1)
                pool.tensor_tensor(rstd[:, :], veps[:, :], neg_half[:, :], ALU.pow).then_inc(step, 1)
                after(2)
                pool.tensor_tensor(newt[:, :], rstd[:, :], rstd[:, :], ALU.mult).then_inc(step, 1)
                after(3)
                pool.tensor_tensor(newt[:, :], newt[:, :], veps[:, :], ALU.mult).then_inc(step, 1)
                after(4)
                pool.tensor_tensor(newt[:, :], newt[:, :], neg_half[:, :], ALU.mult).then_inc(step, 1)
                after(5)
                pool.tensor_tensor(newt[:, :], newt[:, :], three_halves[:, :], ALU.add).then_inc(step, 1)
                after(6)
                pool.tensor_tensor(rstd[:, :], rstd[:, :], newt[:, :], ALU.mult).then_inc(done, 1)

            def divide(b, h):
                for st in range(ST):
                    pool.wait_ge(rinv_done, b * 32 + 4 * h + st + 1)
                    row = pr[:, h % 2, st, :]
                    pool.tensor_tensor(row, row, rinv[:, h % 2, st:st + 1].to_broadcast([P, S]), ALU.mult)\
                        .then_inc(p_done, 1)

            def result_lo(b, pair):
                pool.wait_ge(ahi_done, b * PAIRS + pair + 1)
                pool.tensor_tensor(a_lo[:, pair, :], a32[:, pair % 2, :], a_hi[:, pair, :].bitcast(F32),
                                   ALU.subtract).then_inc(a_done, 1)

            inv_std(0, aggr_done, ln_step, 5, rstd_done)
            divide(0, 0)

            def attention(b, more):
                for h in range(H):
                    if h < H - 1:
                        divide(b, h + 1)
                    elif more:
                        divide(b + 1, 0)
                    if h and h % 2 == 0:
                        result_lo(b, h // 2 - 1)
                    if h == 1 and more:
                        inv_std(b + 1, aggr_done, ln_step, 5, rstd_done)
                result_lo(b, PAIRS - 1)
                pool.wait_ge(xr_loaded, b * 16 + 16)
                for s in range(ST):
                    pool.wait_ge(ring_free, ring(b, out_pos(s, more)))
                    pool.tensor_tensor(xr[:, s, :], xr[:, s, :], t32[:, s % 2, :], ALU.add).then_inc(x_done, 1)

            with pool.Fori(0, B - 1) as b:
                attention(b, True)
            attention(B - 1, False)

            inv_std(0, faggr_done, fln_step, 0, frstd_done)
            pool.wait_ge(fs_loaded, 48)

            def feed_forward(b, more):
                pool.wait_ge(fg_loaded, b * 16 + 16)
                pool.tensor_tensor(gate_bc[:, :], gate_bc[:, :], sdown_bc[:, :], ALU.mult).then_inc(gs_done, 1)
                if more:
                    inv_std(b + 1, faggr_done, fln_step, 0, frstd_done)
                pool.wait_ge(fr_loaded, b * 16 + 16)
                for s in range(ST):
                    pool.wait_ge(y_done, b * ST + ST + s + 1)
                    pool.tensor_tensor(xr[:, s, :], xr[:, s, :], t32[:, s % 2, :], ALU.add).then_inc(fx_done, 1)

            with pool.Fori(0, B - 1) as b:
                feed_forward(b, True)
            feed_forward(B - 1, False)


def kernel(L0_attn_x, L0_attn_Wq, L0_attn_bq, L0_attn_Wk, L0_attn_bk, L0_attn_Wv, L0_attn_bv, L0_attn_Wo,
           L0_attn_bo, L0_ffn_wq_gate, L0_ffn_s_gate, L0_ffn_wq_up, L0_ffn_s_up, L0_ffn_wq_down, L0_ffn_s_down,
           L0_c, L0_wmod):
    import numpy as np
    import concourse.bacc as bacc
    from concourse.bass_utils import run_bass_kernel_spmd

    def tiles_in(w):
        return np.asarray(w).reshape(MT, P, KT, P).transpose(0, 3, 2, 1).reshape(MT, P, F)

    arrays = {
        "x": L0_attn_x,
        "c_t": np.asarray(L0_c).T,
        "wmod": L0_wmod,
        "w_q": L0_attn_Wq, "w_k": L0_attn_Wk, "w_v": L0_attn_Wv, "w_o": L0_attn_Wo,
        "b_q": np.asarray(L0_attn_bq).reshape(PAIRS, P).T,
        "b_k": np.asarray(L0_attn_bk).reshape(PAIRS, P).T,
        "b_v": np.asarray(L0_attn_bv).reshape(H, D).T,
        "b_o": np.asarray(L0_attn_bo).reshape(1, F),
        "w_gate": tiles_in(L0_ffn_wq_gate),
        "w_up": tiles_in(L0_ffn_wq_up),
        "w_down": np.asarray(L0_ffn_wq_down).reshape(F, MT, P).transpose(1, 2, 0),
        "s_gate": np.asarray(L0_ffn_s_gate).reshape(MT, P).T,
        "s_up": np.asarray(L0_ffn_s_up).reshape(MT, P).T,
        "s_down": np.asarray(L0_ffn_s_down).reshape(1, F),
    }
    arrays = {n: np.ascontiguousarray(a) for n, a in arrays.items()}
    nc = bacc.Bacc("TRN2", target_bir_lowering=False, num_devices=1)
    args = {n: nc.dram_tensor(n, a.shape, mybir.dt.from_np(a.dtype), kind="ExternalInput").ap()
            for n, a in arrays.items()}
    out = nc.dram_tensor("out", (B, S, F), F32, kind="ExternalOutput").ap()
    adaln_block(nc, **args, out=out)
    r = run_bass_kernel_spmd(nc, [arrays], core_ids=[0])
    return r.results[0]["out"]
```

```python
from contextlib import ExitStack

import concourse.bass as bass
from concourse import mybir

F32 = mybir.dt.float32
R32 = mybir.dt.float32r
I32 = mybir.dt.int32
ALU = mybir.AluOpType
ACT = mybir.ActivationFunctionType
AXX = mybir.AxisListType.X

P = 128
B, S, F = 8, 512, 512
H, D = 8, 64
HID = 1408
KT = F // P
ST = S // P
PAIRS = H // 2
MT = HID // P
ZERO_POINT = 128.0
EPS = 1e-5
QSCALE = 8.0 ** -0.5
SA, CA, GA, SB, CB, GB = range(6)

UNITS = MT + 3

RING = H * ST + ST


def turn_pos(h, j):
    return ST * h + j


def out_pos(s):
    return H * ST + s


def filler_of(h):
    if h < 4:
        return 0, 2 + h // 2, h % 2
    return 1, (h - 4) // 2, h % 2


def adaln_block(nc, x, c_t, wmod, w_q, w_k, w_v, w_o, b_q, b_k, b_v, b_o, w_gate, w_up, w_down,
                s_gate, s_up, s_down, out):
    x1_dram = nc.dram_tensor("x1_scratch", [B, S, F], F32, kind="Internal").ap()
    gates_dram = nc.dram_tensor("gates_scratch", [2, B, F], F32, kind="Internal").ap()

    def tokens(a, b):
        return a[b, :, :].rearrange("(t p) f -> p t f", p=P)

    ctx = ExitStack()
    with ctx:
        at = [0]
        place_of = {}

        def sb(name, shape, dt=F32):
            n = 4
            for d in shape[1:]:
                n *= d
            t = nc.alloc_sbuf_tensor_at(name, shape, dt, offset=at[0])
            place_of[t.name] = at[0]
            at[0] += (n + 31) // 32 * 32
            assert at[0] <= TOP, (name, at[0], TOP)
            return t

        at[0] = (nc.sbuf_base + 31) // 32 * 32
        TOP = at[0] + nc.sbuf_bytes_remaining // 32 * 32 - 32

        def as_f32(t, name, shape):
            return nc.alloc_sbuf_tensor_at(name, shape, F32, offset=place_of[t.name])

        def sem(name):
            return ctx.enter_context(nc.semaphore(name))

        ident = sb("ident", [P, P])
        modc = sb("modc", [P, 4, KT, B])
        neg_half = sb("neg_half", [P, ST])
        three_halves = sb("three_halves", [P, ST])
        eps_t = sb("eps_t", [P, ST])
        stats = sb("stats", [P, ST, 6])
        mv = sb("mv", [P, ST, 2])
        veps = sb("veps", [P, ST])
        rstd = sb("rstd", [P, ST])
        newt = sb("newt", [P, ST])
        h32 = sb("h32", [P, 2, S])
        xn = sb("xn", [P, ST, F])
        xr = sb("xr", [P, ST, F])
        hT_hi = sb("hT_hi", [P, KT, S], R32)
        hT_lo = sb("hT_lo", [P, KT, S], R32)
        gate_bc = sb("gate_bc", [P, F])
        t32 = sb("t32", [P, 2, F])
        sg_half = sb("sg_half", [P, MT])
        su_col = sb("su_col", [P, MT])
        sgu_half = sb("sgu_half", [P, MT])
        both = at[0]
        Wp_hi = sb("Wp_hi", [P, 3, KT, F], R32)
        Wp_lo = sb("Wp_lo", [P, 3, KT, F], R32)
        projections_end = at[0]
        bqkv = sb("bqkv", [P, 3, PAIRS])
        bv_h = sb("bv_h", [D, H])
        c_sb = sb("c_sb", [P, KT, B])
        c_th = sb("c_th", [P, KT, B])
        c_silu = sb("c_silu", [P, KT, B])
        negmax = sb("negmax", [P, 2, ST])
        ssum = sb("ssum", [P, 2, ST])
        rinv = sb("rinv", [P, 2, ST])
        bo_hi = sb("bo_hi", [1, F], R32)
        bo_lo = sb("bo_lo", [1, F], R32)
        ones_f = sb("ones_f", [1, P])
        ones_r = sb("ones_r", [1, P], R32)
        Wo_hi = sb("Wo_hi", [P, KT, F], R32)
        Wo_lo = sb("Wo_lo", [P, KT, F], R32)
        W_hi = [Wp_hi[:, i, :, :] for i in range(3)] + [Wo_hi[:, :, :]]
        W_lo = [Wp_lo[:, i, :, :] for i in range(3)] + [Wo_lo[:, :, :]]
        qs = sb("qs", [P, 2, 2, S], R32)
        kh = sb("kh", [P, 2, 2, S], R32)
        kl = sb("kl", [P, 2, S], R32)
        v_sb = sb("v_sb", [P, ST, H, 2, D], R32)
        pr = sb("pr", [P, 2, ST, S])
        pt_hi = sb("pt_hi", [P, ST, S], R32)
        pt_lo = sb("pt_lo", [P, ST, S], R32)
        c32 = sb("c32", [D, S])
        a32 = sb("a32", [P, 2, S])
        bo_f = h32[0:1, 0, :]
        a_hi = sb("a_hi", [P, PAIRS, S], R32)
        a_lo = sb("a_lo", [P, PAIRS, S], R32)
        g_tmp = t32
        g_rows = [h32[0:B, g, :] for g in range(2)]
        pt_hi_f = as_f32(pt_hi, "pt_hi_f", [P, ST, S])
        pt_lo_f = as_f32(pt_lo, "pt_lo_f", [P, ST, S])
        a_hi_f = as_f32(a_hi, "a_hi_f", [P, PAIRS, S])
        a_lo_f = as_f32(a_lo, "a_lo_f", [P, PAIRS, S])
        at[0] = both
        w_raw = sb("w_raw", [P, 2, 3, F], I32)
        EARLY = (projections_end - at[0]) // (6 * F * 4)
        assert EARLY >= 2
        w_ff = sb("w_ff", [P, MT, 6, F], R32)
        g_hi = sb("g_hi", [P, 2, S], R32)
        g_lo = sb("g_lo", [P, 2, S], R32)
        tanh_sb = sb("tanh_sb", [P, S])
        a_sb = sb("a_sb", [P, S])
        g32 = sb("g32", [P, S])
        lo_square = sb("lo_square", [P, F])
        lo_sums = sb("lo_sums", [P, 3 * MT])
        lo_sum = sb("lo_sum", [P, 1])
        lo_row = sb("lo_row", [1, P])
        lo_all = sb("lo_all", [1, 1])
        lo_flag = sb("lo_flag", [1, 1], I32)
        sdown_bc = sb("sdown_bc", [P, F])

        psum = nc.alloc_psum_tensor("banks", [P, 8, 512], F32)
        SC = [psum[:, i, :] for i in range(4)]
        TB = [psum[:, 4 + i, :] for i in range(2)]
        PVB = psum[:, 6, :]
        PJ = psum[:, 7, :]

        const_ready = sem("const_ready")
        small_loaded = sem("small_loaded")
        c_loaded = sem("c_loaded")
        wmod_loaded = [sem(f"wmod{n}_loaded") for n in range(6)]
        w_loaded = [sem(f"w_{c}_loaded") for c in "qkvo"]
        silu_step = sem("silu_step")
        bias_ready = sem("bias_ready")
        mod_mm = sem("mod_mm")
        mod_col = sem("mod_col")
        gate_step = sem("gate_step")
        gate_rows = sem("gate_rows")
        gates_stored = sem("gates_stored")
        w_hi_done = sem("w_hi_done")
        w_lo_done = sem("w_lo_done")
        xn_loaded = sem("xn_loaded")
        xr_loaded = sem("xr_loaded")
        gate_loaded = sem("gate_loaded")
        bn_done = sem("bn_done")
        aggr_begun = sem("aggr_begun")
        aggr_done = sem("aggr_done")
        ln_step = sem("ln_step")
        rstd_done = sem("rstd_done")
        ln_done = sem("ln_done")
        ring_ready = sem("ring_ready")
        ring_free = sem("ring_free")
        pj_ready = sem("pj_ready")
        pj_hi = sem("pj_hi")
        pj_done = sem("pj_done")
        h32_done = sem("h32_done")
        h_hi = sem("h_hi")
        h_done = sem("h_done")
        k_copied = sem("k_copied")
        norm_turned = sem("norm_turned")
        v_ready = sem("v_ready")
        v_hi = sem("v_hi")
        v_done = sem("v_done")
        s_ready = sem("s_ready")
        max_done = sem("max_done")
        exp_done = sem("exp_done")
        rinv_done = sem("rinv_done")
        p_done = sem("p_done")
        pt_hi_done = sem("pt_hi_done")
        pv_ready = sem("pv_ready")
        c_done = sem("c_done")
        pv_free = sem("pv_free")
        ahi_done = sem("ahi_done")
        a_done = sem("a_done")
        x_done = sem("x_done")
        x1_stored = sem("x1_stored")
        fs_loaded = sem("fs_loaded")
        fs_step = sem("fs_step")
        wraw_loaded = [sem(f"wraw{i}_loaded") for i in range(2)]
        sdown_loaded = sem("sdown_loaded")
        whi_done = sem("whi_done")
        wlo_done = sem("wlo_done")
        squares_done = sem("squares_done")
        lo_summed = sem("lo_summed")
        lo_turned = sem("lo_turned")
        lo_known = sem("lo_known")
        fr_loaded = sem("fr_loaded")
        fg_loaded = sem("fg_loaded")
        unit_ready = sem("unit_ready")
        unit_free = sem("unit_free")
        fh_hi = sem("fh_hi")
        fh_done = sem("fh_done")
        tanh_done = sem("tanh_done")
        a_step = sem("a_step")
        ghi_done = sem("ghi_done")
        g_done = sem("g_done")
        d_done = sem("d_done")
        gs_done = sem("gs_done")
        y_done = sem("y_done")
        fx_done = sem("fx_done")
        stored = sem("stored")

        block = ctx.enter_context(nc.Block())

        def ring(b, pos):
            return b * RING + pos + 1

        w_stage = [pt_hi_f[:, :, :], pt_lo_f[:, :, :], xr[:, :, :], a_hi_f[:, :, :]]
        wmod_stage = [pr[:, 0, :, :], pr[:, 1, :, :], a_lo_f[:, :, :], pt_hi_f[:, :, :], pt_lo_f[:, :, :],
                      pr[:, 1, :, :]]
        COLS = {SA: 0, CA: 1, SB: 2, CB: 3}

        @block.sync
        def _(sp):
            def load_w(n):
                sp.dma_start(w_stage[n], (w_q, w_k, w_v, w_o)[n].rearrange("(k p) n -> p k n", p=P))\
                    .then_inc(w_loaded[n], 16)

            def load_wmod(n):
                sp.dma_start(wmod_stage[n], wmod[:, n * F:(n + 1) * F].rearrange("(k p) n -> p k n", p=P))\
                    .then_inc(wmod_loaded[n], 16)

            sp.dma_start(c_sb[:, :, :], c_t.rearrange("(k p) b -> p k b", p=P)).then_inc(c_loaded, 16)
            sp.dma_start(xn[:, :, :], tokens(x, 0)).then_inc(xn_loaded, 16)
            load_wmod(SA)
            load_wmod(CA)
            for j, bias in enumerate((b_q, b_k)):
                sp.dma_start(bqkv[:, j, :], bias).then_inc(small_loaded, 16)
            sp.dma_start(bv_h[:, :], b_v).then_inc(small_loaded, 16)
            sp.dma_start(bo_f, b_o).then_inc(small_loaded, 16)
            load_w(0)
            load_w(1)
            load_w(2)
            load_wmod(GA)
            load_w(3)
            def stores(b):
                for s in range(ST):
                    sp.wait_ge(x_done, b * ST + s + 3)
                    sp.dma_start(x1_dram[b, s * P:(s + 1) * P, :], xr[:, s, :]).then_inc(x1_stored, 16)

            def load_xn(i, src, b):
                sp.wait_ge(norm_turned, i * KT)
                sp.dma_start(xn[:, :, :], tokens(src, b)).then_inc(xn_loaded, 16)

            def attention(b, later):
                if later == 2:
                    load_xn(b + 2, x, b + 2)
                elif later == 1:
                    load_xn(B, x1_dram, 0)
                if not later:
                    sp.wait_ge(pj_ready, B * H)
                    ff_tile(0)
                    ff_tile(1)
                    load_xn(B + 1, x1_dram, 1)
                stores(b)
                if later:
                    sp.wait_ge(x1_stored, b * 64 + 64)
                    sp.dma_start(xr[:, :, :], tokens(x, b + 1)).then_inc(xr_loaded, 16)
                    sp.dma_start(gate_bc[:, :], gates_dram[0, bass.ds(b + 1, 1), :].partition_broadcast(P))\
                        .then_inc(gate_loaded, 16)

            def ff_tile(m):
                for j, w in enumerate((w_gate, w_up, w_down)):
                    sp.dma_start(w_raw[:, m % 2, j, :], w[m, :, :]).then_inc(wraw_loaded[m % 2], 16)

            sp.dma_start(sg_half[:, :], s_gate).then_inc(fs_loaded, 16)
            sp.dma_start(su_col[:, :], s_up).then_inc(fs_loaded, 16)
            sp.wait_ge(w_lo_done, 1)
            load_wmod(SB)
            sp.wait_ge(mod_mm, 2)
            load_wmod(GB)
            sp.wait_ge(w_lo_done, 2)
            load_wmod(CB)
            load_xn(1, x, 1)
            sp.wait_ge(w_lo_done, 3)
            sp.dma_start(xr[:, :, :], tokens(x, 0)).then_inc(xr_loaded, 16)
            for g in range(2):
                sp.wait_ge(gate_rows, g + 1)
                sp.dma_start(gates_dram[g, :, :], g_rows[g]).then_inc(gates_stored, 16)
            sp.wait_ge(gates_stored, 32)
            sp.dma_start(gate_bc[:, :], gates_dram[0, 0:1, :].partition_broadcast(P)).then_inc(gate_loaded, 16)
            with sp.Fori(0, B - 2) as b:
                attention(b, 2)
            attention(B - 2, 1)
            attention(B - 1, 0)
            sp.wait_ge(x1_stored, B * 64)

            sp.dma_start(xr[:, :, :], tokens(x1_dram, 0)).then_inc(fr_loaded, 16)
            sp.dma_start(gate_bc[:, :], gates_dram[1, 0:1, :].partition_broadcast(P)).then_inc(fg_loaded, 16)
            for m in range(2, MT):
                sp.wait_ge(wlo_done, m - 1)
                ff_tile(m)
                if m == 2:
                    sp.dma_start(sdown_bc[:, :], s_down.partition_broadcast(P)).then_inc(sdown_loaded, 16)
            sp.wait_ge(lo_summed, 1)
            sp.dma_start(lo_row[0:1, :], lo_sum[:, :]).then_inc(lo_turned, 16)

            def out_stores(b):
                for s in range(ST):
                    sp.wait_ge(fx_done, b * ST + s + 3)
                    sp.dma_start(out[b, s * P:(s + 1) * P, :], xr[:, s, :]).then_inc(stored, 16)

            def turn_over(b):
                out_stores(b)
                sp.wait_ge(stored, b * 64 + 64)
                sp.dma_start(xr[:, :, :], tokens(x1_dram, b + 1)).then_inc(fr_loaded, 16)
                sp.dma_start(gate_bc[:, :], gates_dram[1, bass.ds(b + 1, 1), :].partition_broadcast(P))\
                    .then_inc(fg_loaded, 16)

            turn_over(0)
            with sp.Fori(1, B - 1) as b:
                sp.wait_ge(unit_ready, b * UNITS)
                sp.dma_start(xn[:, :, :], tokens(x1_dram, b + 1)).then_inc(xn_loaded, 16)
                turn_over(b)
            out_stores(B - 1)
            sp.wait_ge(stored, B * 64)

        @block.tensor
        def _(pe):
            def turn_norm(f, bank):
                for t in range(ST):
                    mm = pe.transpose(bank[:, t * P:(t + 1) * P], xn[:, t, f * P:(f + 1) * P], ident[:, :])
                return mm

            def project(bank, w, m, steps=range(12), ready=None):
                for i in steps:
                    k, part = divmod(i, 3)
                    if part == 0 and ready is not None:
                        ready(k)
                    lhs = (W_lo if part == 2 else W_hi)[w][:, k, m * P:(m + 1) * P]
                    rhs = (hT_lo if part == 1 else hT_hi)[:, k, :]
                    mm = pe.matmul(bank, lhs, rhs, start=(i == 0), stop=(i == 11))
                return mm

            def scores(b, h, sts, first=False):
                pb, w = h // 2 % 2, h % 2
                if h == 1 and sts[0] == 0:
                    pe.wait_ge(v_done, b * ST + ST)
                if sts[0] == 0:
                    pe.wait_ge(pj_done, b * H + 2 * (h // 2) + 2)
                    pe.wait_ge(k_copied, b * PAIRS + h // 2 + 1)
                lo = slice(0, D) if w == 0 else slice(D, P)
                for st in sts:
                    if not first:
                        pe.wait_ge(exp_done, b * 32 + 4 * h + st - 3)
                    cols = slice(st * P, (st + 1) * P)
                    pe.matmul(SC[st], qs[:, pb, w, cols], kh[:, pb, w, :], start=True, stop=False)
                    pe.matmul(SC[st], qs[lo, pb, w, cols], kl[lo, pb, :], start=False, stop=True)\
                        .then_inc(s_ready, 1)

            def turn(b, h, j):
                n = turn_pos(h, j)
                pe.wait_ge(ring_free, ring(b, n))
                if j == 0:
                    pe.wait_ge(p_done, b * 32 + 4 * h + 4)
                for st in range(ST):
                    mm = pe.transpose(TB[n % 2][:, st * P:(st + 1) * P],
                                      pr[:, h % 2, st, j * P:(j + 1) * P], ident[:, :])
                mm.then_inc(ring_ready, 1)

            def pv(b, h, j):
                if j == 0:
                    pe.wait_ge(pv_free, b * H + h + 1)
                pe.wait_ge(ring_free, ring(b, turn_pos(h, j)) + 2)
                lhs = v_sb[:, j, h, :, :].rearrange("p a d -> p (a d)")
                pe.matmul(PVB, lhs, pt_hi[:, j, :], start=(j == 0), stop=False)
                mm = pe.matmul(PVB, lhs, pt_lo[:, j, :], start=False, stop=(j == ST - 1))
                if j == ST - 1:
                    mm.then_inc(pv_ready, 1)

            def values(t, bank):
                for i in range(12):
                    k, part = divmod(i, 3)
                    lhs = (hT_lo if part == 1 else hT_hi)[:, k, t * P:(t + 1) * P]
                    rhs = (W_lo if part == 2 else W_hi)[2][:, k, :]
                    mm = pe.matmul(bank, lhs, rhs, start=(i == 0), stop=(i == 11))
                return mm

            def output(s, bank):
                pe.matmul(bank, ones_r[:, :], bo_hi[:, :], start=True, stop=False)
                pe.matmul(bank, ones_r[:, :], bo_lo[:, :], start=False, stop=False)
                for i in range(12):
                    k, part = divmod(i, 3)
                    lhs = (a_lo if part == 1 else a_hi)[:, k, s * P:(s + 1) * P]
                    rhs = (W_lo if part == 2 else W_hi)[3][:, k, :]
                    mm = pe.matmul(bank, lhs, rhs, start=False, stop=(i == 11))
                return mm

            def mod_columns(kind):
                pe.wait_ge(wmod_loaded[kind], 16)
                bank = SC[COLS[kind]]
                for f in range(KT):
                    for k in range(KT):
                        mm = pe.matmul(bank[:, f * B:(f + 1) * B], wmod_stage[kind][:, k, f * P:(f + 1) * P],
                                       c_silu[:, k, :], start=(k == 0), stop=(k == KT - 1))
                mm.then_inc(mod_mm, 1)

            def mod_rows(kind):
                pe.wait_ge(wmod_loaded[kind], 16)
                for k in range(KT):
                    mm = pe.matmul(PVB[0:B, :], c_silu[:, k, :], wmod_stage[kind][:, k, :],
                                   start=(k == 0), stop=(k == KT - 1))
                mm.then_inc(mod_mm, 1)

            def first_projection(i):
                if i:
                    pe.wait_ge(pj_done, i)
                if i < 2:
                    pe.wait_ge(w_lo_done, i + 1)
                project(PJ, i % 2, i // 2, ready=lambda k: pe.wait_ge(h_done, k + 1)).then_inc(pj_ready, 1)

            def first_values(t):
                if t == 0:
                    pe.wait_ge(w_lo_done, 3)
                if t >= 2:
                    pe.wait_ge(v_done, t - 1)
                values(t, TB[t % 2]).then_inc(v_ready, 1)

            pe.wait_ge(silu_step, 3)
            mod_columns(SA)
            mod_columns(CA)
            pe.wait_ge(const_ready, 1)
            for f in range(KT):
                if f == 0:
                    pe.wait_ge(ln_done, ST)
                if f >= 2:
                    pe.wait_ge(h32_done, f - 1)
                turn_norm(f, TB[f % 2]).then_inc(norm_turned, 1)
            first_projection(0)
            first_projection(1)
            first_values(0)
            first_values(1)
            scores(0, 0, range(ST), first=True)
            first_projection(2)
            mod_rows(GA)
            first_values(2)
            first_projection(3)
            pe.wait_ge(exp_done, ST)
            mod_columns(SB)
            mod_columns(CB)
            pe.wait_ge(gate_rows, 1)
            mod_rows(GB)
            first_values(3)
            pe.wait_ge(mod_col, 4)
            pe.wait_ge(gate_rows, 2)
            pe.wait_ge(w_lo_done, 4)

            def filler(b, h, steps):
                nxt, pair, qk = filler_of(h)
                bb = b + nxt
                use = bb * H + 2 * pair + qk
                if steps[0] == 0:
                    pe.wait_ge(pj_done, use)
                mm = project(PJ, qk, pair, steps,
                             ready=(lambda k: pe.wait_ge(h_done, b * KT + KT + k + 1)) if h == 4 else None)
                if steps[-1] == 11:
                    mm.then_inc(pj_ready, 1)

            pe.wait_ge(v_done, ST)

            def norm_turn(b, f):
                if f == 0:
                    pe.wait_ge(ln_done, b * ST + 2 * ST)
                    pe.wait_ge(pj_done, b * H + 8)
                else:
                    pe.wait_ge(h32_done, b * KT + KT + f)
                turn_norm(f, PJ).then_inc(norm_turned, 1)

            def attention(b, more):
                for h in range(H):
                    norm = h == 4
                    fill = (h < 4 or more) and not norm
                    after = (b, h + 1) if h < H - 1 else (b + 1, 0)
                    last = h == H - 1 and not more
                    if not last:
                        scores(*after, range(0, 2))
                    if norm:
                        norm_turn(b, 0)
                    if h:
                        pv(b, h - 1, 2)
                    if fill:
                        filler(b, h, range(0, 4))
                    turn(b, h, 0)
                    if norm:
                        norm_turn(b, 1)
                    if h:
                        pv(b, h - 1, 3)
                    if not last:
                        scores(*after, range(2, 4))
                    if fill:
                        filler(b, h, range(4, 8))
                    turn(b, h, 1)
                    if norm:
                        norm_turn(b, 2)
                    if fill:
                        filler(b, h, range(8, 10))
                    pv(b, h, 0)
                    turn(b, h, 2)
                    if fill:
                        filler(b, h, range(10, 12))
                    if norm:
                        norm_turn(b, 3)
                    pv(b, h, 1)
                    turn(b, h, 3)
                    if norm and more:
                        pe.wait_ge(h32_done, b * KT + 2 * KT)
                        filler(b, h, range(0, 12))
                for t in range(ST if more else 0):
                    pe.wait_ge(exp_done, b * 32 + 32 + t + 1)
                    values(t, SC[t]).then_inc(v_ready, 1)
                    if t < 2:
                        pv(b, H - 1, 2 + t)
                if not more:
                    pv(b, H - 1, 2)
                    pv(b, H - 1, 3)
                for s in range(ST):
                    n = out_pos(s)
                    pe.wait_ge(ring_free, ring(b, n))
                    if s == 0:
                        pe.wait_ge(a_done, b * PAIRS + PAIRS)
                    output(s, TB[n % 2]).then_inc(ring_ready, 1)

            with pe.Fori(0, B - 1) as b:
                attention(b, True)
            attention(B - 1, False)

            G = [psum[:, 0, :], psum[:, 2, :]]
            U = [psum[:, 1, :], psum[:, 3, :]]
            Y = [psum[:, 4 + s, :] for s in range(ST)]
            NORM_UNITS = [(0, 1), (2,), (3,)]

            def ff_norm(b, u):
                n = b * UNITS + MT + u
                pe.wait_ge(unit_free, n - 1)
                for f in NORM_UNITS[u]:
                    bank = (G if f in (0, 2, 3) else U)[(MT + u) % 2]
                    for t in range(ST):
                        mm = pe.transpose(bank[:, t * P:(t + 1) * P], xn[:, t, f * P:(f + 1) * P], ident[:, :])
                mm.then_inc(unit_ready, 1)

            def gate_up(b, m, bi, parts):
                u = m % 2
                if bi or m >= 2:
                    pe.wait_ge(unit_free, b * UNITS + m - 1)
                if bi == 0:
                    pe.wait_ge(wlo_done, m + 1)
                for j, bank in ((0, G[u]), (2, U[u])):
                    for i in range(KT * parts):
                        k, part = divmod(i, parts)
                        if m == 0 and part == 0 and bank is G[u]:
                            if bi == 0:
                                pe.wait_ge(h_done, B * KT + k + 1)
                            else:
                                pe.wait_ge(fh_done, b * KT - KT + k + 1)
                        mm = pe.matmul(bank, w_ff[:, m, j + part // 2, k * P:(k + 1) * P],
                                       (hT_lo if part == 1 else hT_hi)[:, k, :],
                                       start=(i == 0), stop=(i == KT * parts - 1))
                mm.then_inc(unit_ready, 1)

            def down(b, m, bi, parts):
                pe.wait_ge(g_done, b * MT + m + 1)
                for s in range(ST):
                    if m == 0:
                        if s == 0 and bi == 0:
                            pe.wait_ge(ring_free, ring(B - 1, out_pos(ST - 1)) + 2)
                        pe.wait_ge(y_done, b * ST + s + 1)
                    cols = slice(s * P, (s + 1) * P)
                    pe.matmul(Y[s], g_hi[:, m % 2, cols], w_ff[:, m, 4, :], start=(m == 0), stop=False)
                    last = m == MT - 1
                    mm = pe.matmul(Y[s], g_lo[:, m % 2, cols], w_ff[:, m, 4, :], start=False,
                                   stop=last and parts == 2)
                    if parts == 3:
                        mm = pe.matmul(Y[s], g_hi[:, m % 2, cols], w_ff[:, m, 5, :], start=False, stop=last)
                mm.then_inc(d_done, 1)

            def feed_forward(b, bi, more, parts):
                for m in range(MT):
                    gate_up(b, m, bi, parts)
                    if m:
                        down(b, m - 1, bi, parts)
                if more:
                    pe.wait_ge(ln_done, (b + B + 1) * ST + ST)
                    for u in range(3):
                        ff_norm(b, u)
                down(b, MT - 1, bi, parts)

            feed_forward(0, 0, True, 3)

            def other_batches(parts):
                with pe.Fori(1, B - 1) as b:
                    feed_forward(b, 1, True, parts)
                feed_forward(B - 1, B - 1, False, parts)

            pe.wait_ge(lo_known, 1)
            with pe.If(pe.value_load(lo_flag[0:1, 0:1]) != 0):
                other_batches(3)
            with pe.Else():
                other_batches(2)
            pe.end_ifs()

        @block.scalar
        def _(act):
            act.wait_ge(c_loaded, 16)
            act.activation(c_th[:, :, :], c_sb[:, :, :], ACT.Tanh, scale=0.5).then_inc(silu_step, 1)
            act.wait_ge(small_loaded, 16 * 4)
            act.mul(bqkv[:, 0, :], bqkv[:, 0, :], QSCALE).then_inc(bias_ready, 1)
            act.activation(bo_hi[:, :], bo_f, ACT.Copy).then_inc(bias_ready, 1)

            def split_hi(w):
                act.wait_ge(w_loaded[w], 16)
                act.activation(W_hi[w], w_stage[w], ACT.Copy,
                               scale=QSCALE if w == 0 else 1.0).then_inc(w_hi_done, 1)

            def modulate(b, f, bank, kind=0, col=None):
                col = b if col is None else col
                act.wait_ge(norm_turned, b * KT + f + 1)
                if not (isinstance(b, int) and b == 0):
                    if f == 0:
                        act.wait_ge(gates_stored, 32)
                if not (isinstance(b, int) and b == 0 and f < 2):
                    act.wait_ge(h_done, b * KT + f - 1)
                act.activation(h32[:, f % 2, :], bank, ACT.Identity, bias=modc[:, kind, f, bass.ds(col, 1)],
                               scale=modc[:, kind + 1, f, bass.ds(col, 1)]).then_inc(h32_done, 1)

            def proj_hi(b, pair, qk):
                act.wait_ge(pj_ready, b * H + 2 * pair + qk + 1)
                for w, src in ((0, slice(0, D)), (1, slice(D, P))):
                    a = act.activation((qs, kh)[qk][src, pair % 2, w, :], PJ[src, :], ACT.Identity,
                                       bias=bqkv[src, qk, pair:pair + 1], scale=1.0)
                a.then_inc(pj_hi, 1)

            def k_copy(b, pair):
                act.wait_ge(pj_hi, b * H + 2 * pair + 2)
                for w, src, dst in ((0, slice(0, D), slice(D, P)), (1, slice(D, P), slice(0, D))):
                    a = act.activation(kh[dst, pair % 2, w, :], kh[src, pair % 2, w, :].bitcast(F32), ACT.Copy)
                a.then_inc(k_copied, 1)

            def exps(b, h, st):
                act.wait_ge(max_done, b * 32 + 4 * h + st + 1)
                act.activation(pr[:, h % 2, st, :], SC[st], ACT.Exp, bias=negmax[:, h % 2, st:st + 1],
                               scale=1.0, accum_out=ssum[:, h % 2, st:st + 1]).then_inc(exp_done, 1)

            def weights_hi(b, h, j):
                n = turn_pos(h, j)
                act.wait_ge(ring_ready, ring(b, n))
                act.activation(pt_hi[:, j, :], TB[n % 2], ACT.Copy).then_inc(pt_hi_done, 1)

            def lower_half(b, h):
                act.wait_ge(pv_ready, b * H + h + 1)
                act.activation(c32[:, :], PVB[D:P, :], ACT.Copy).then_inc(c_done, 1)

            def v_his(b, t, bank):
                act.wait_ge(v_ready, b * ST + t + 1)
                act.activation(v_sb[:, t, :, 0, :], bank.rearrange("p (h d) -> p h d", d=D), ACT.Copy)\
                    .then_inc(v_hi, 1)

            def weights_split(m):
                act.wait_ge(wraw_loaded[m % 2], 48 * (m // 2 + 1))
                for j in range(3):
                    a = act.activation(w_ff[:, m, 2 * j, :], w_raw[:, m % 2, j, :], ACT.Copy, bias=-ZERO_POINT)
                a.then_inc(whi_done, 1)

            act.wait_ge(bias_ready, 4)
            split_hi(0)
            split_hi(1)
            act.wait_ge(mod_col, 2)
            for f in range(KT):
                modulate(0, f, TB[f % 2])
            proj_hi(0, 0, 0)
            split_hi(2)
            proj_hi(0, 0, 1)
            k_copy(0, 0)
            v_his(0, 0, TB[0])
            v_his(0, 1, TB[1])
            for st in range(ST):
                exps(0, 0, st)
            proj_hi(0, 1, 0)
            v_his(0, 2, TB[0])
            split_hi(3)
            proj_hi(0, 1, 1)
            k_copy(0, 1)
            v_his(0, 3, TB[1])

            def attention(b, more):
                for h in range(H):
                    norm = h == 4
                    after = (b, h + 1) if h < H - 1 else (b + 1, 0)
                    last = h == H - 1 and not more

                    def next_exps(st):
                        if not last:
                            exps(*after, st)

                    def next_norm(f):
                        if norm:
                            if more:
                                modulate(b + 1, f, PJ)
                            else:
                                modulate(B, f, PJ, kind=2, col=0)

                    if h and h != 5:
                        weights_hi(b, h - 1, 3)
                    next_exps(0)
                    next_norm(0)
                    next_exps(1)
                    weights_hi(b, h, 0)
                    next_norm(1)
                    if h:
                        lower_half(b, h - 1)
                    next_exps(2)
                    weights_hi(b, h, 1)
                    next_norm(2)
                    next_exps(3)
                    if norm:
                        weights_hi(b, h, 2)
                        next_norm(3)
                        weights_hi(b, h, 3)
                    if h < 4 or more:
                        nxt, pair, qk = filler_of(h)
                        proj_hi(b + nxt, pair, qk)
                    if not norm:
                        weights_hi(b, h, 2)
                    if h % 2 and (h < 4 or more):
                        k_copy(b + nxt, pair)
                weights_hi(b, H - 1, 3)
                if not more:
                    act.wait_ge(fs_step, 2)
                    weights_split(0)
                if more:
                    v_his(b + 1, 0, SC[0])
                lower_half(b, H - 1)
                for t in range(1, ST if more else 0):
                    v_his(b + 1, t, SC[t])
                if not more:
                    weights_split(1)

            with act.Fori(0, B - 1) as b:
                attention(b, True)
            attention(B - 1, False)

            def squares(m):
                act.wait_ge(wlo_done, m + 1)
                for j in range(3):
                    if m or j:
                        act.wait_ge(squares_done, 3 * m + j)
                    act.activation(lo_square[:, :], w_ff[:, m, 2 * j + 1, :].bitcast(F32), ACT.Square,
                                   accum_out=lo_sums[:, 3 * m + j:3 * m + j + 1]).then_inc(squares_done, 1)

            def ff_norm_hi(b, f):
                act.wait_ge(unit_free, b * UNITS + MT + (1, 1, 2, 3)[f])
                act.activation(hT_hi[:, f, :], h32[:, f % 2, :], ACT.Copy).then_inc(fh_hi, 1)

            G = [psum[:, 0, :], psum[:, 2, :]]

            def feed_forward(b, bi, more):
                for m in range(MT):
                    if bi == 0 and 2 <= m + 1 < MT:
                        weights_split(m + 1)
                    act.wait_ge(unit_ready, b * UNITS + m + 1)
                    act.activation(tanh_sb[:, :], G[m % 2], ACT.Tanh, scale=sg_half[:, m:m + 1])\
                        .then_inc(tanh_done, 1)
                    act.wait_ge(unit_free, b * UNITS + m + 1)
                    if bi or m >= 2:
                        act.wait_ge(d_done, b * MT + max(m - 1, 0))
                    act.activation(g_hi[:, m % 2, :], g32[:, :], ACT.Copy).then_inc(ghi_done, 1)
                    if bi == 0:
                        squares(m)
                if more:
                    for f in range(KT):
                        ff_norm_hi(b, f)

            feed_forward(0, 0, True)
            with act.Fori(1, B - 1) as b:
                feed_forward(b, 1, True)
            feed_forward(B - 1, B - 1, False)


        @block.vector
        def _(dve):
            def norm_stats(b, t):
                if t == 0:
                    dve.wait_ge(xn_loaded, b * 16 + 16)
                dve.bn_stats(stats[:, t, :], xn[:, t, :]).then_inc(bn_done, 1)

            def norm_aggr(b):
                dve.wait_ge(bn_done, b * ST + ST)
                dve.sem_inc(aggr_begun, 1)
                for t in range(ST):
                    dve.bn_aggr(mv[:, t, :], stats[:, t, :]).then_inc(aggr_done, 1)

            def norm_scale(b, t):
                if t == 0:
                    dve.wait_ge(rstd_done, b + 1)
                dve.tensor_scalar(xn[:, t, :], xn[:, t, :], mv[:, t, 0:1], rstd[:, t:t + 1],
                                  ALU.subtract, ALU.mult).then_inc(ln_done, 1)

            def norm_tokens(b):
                for t in range(ST):
                    norm_stats(b, t)
                norm_aggr(b)
                for t in range(ST):
                    norm_scale(b, t)

            def modulate(f, b, kind, bank):
                return dve.tensor_scalar(h32[:, f % 2, :], bank, modc[:, kind + 1, f, bass.ds(b, 1)],
                                         modc[:, kind, f, bass.ds(b, 1)], ALU.mult, ALU.add)

            def norm_lo(f):
                return dve.tensor_tensor(hT_lo[:, f, :], h32[:, f % 2, :], hT_hi[:, f, :].bitcast(F32),
                                         ALU.subtract)

            def norm_hi(b, f):
                dve.wait_ge(h32_done, b * KT + f + 1)
                dve.tensor_copy(hT_hi[:, f, :], h32[:, f % 2, :]).then_inc(h_hi, 1)

            dve.wait_ge(silu_step, 1)
            dve.scalar_tensor_tensor(c_silu[:, :, :], c_th[:, :, :], 1.0, c_sb[:, :, :], ALU.add, ALU.mult)\
                .then_inc(silu_step, 1)
            dve.wait_ge(silu_step, 2)
            dve.tensor_scalar(c_silu[:, :, :], c_silu[:, :, :], 0.5, None, ALU.mult).then_inc(silu_step, 1)
            norm_tokens(0)
            dve.wait_ge(bias_ready, 2)
            dve.tensor_tensor(bo_lo[:, :], bo_f, bo_hi[:, :].bitcast(F32), ALU.subtract).then_inc(bias_ready, 1)
            dve.tensor_copy(ones_r[:, :], ones_f[:, :]).then_inc(bias_ready, 1)

            def mod_columns(kind, n):
                dve.wait_ge(mod_mm, n)
                turned = SC[COLS[kind]][:, 0:KT * B].rearrange("p (k b) -> p k b", b=B)
                dve.tensor_scalar(modc[:, COLS[kind], :, :], turned, float(kind in (CA, CB)), None, ALU.add)\
                    .then_inc(mod_col, 1)

            def gate(g, n):
                bank = PVB[0:B, :]
                dve.wait_ge(mod_mm, n)
                dve.tensor_scalar(g_tmp[0:B, 0, :], bank, 0.0, 2.0, ALU.is_ge, ALU.mult).then_inc(gate_step, 1)
                dve.tensor_scalar(g_tmp[0:B, 1, :], bank, -1.0, 0.25, ALU.mult, ALU.max).then_inc(gate_step, 1)
                dve.wait_ge(gate_step, 3 * g + 2)
                dve.tensor_tensor(g_tmp[0:B, 1, :], bank, g_tmp[0:B, 1, :], ALU.max).then_inc(gate_step, 1)
                dve.wait_ge(gate_step, 3 * g + 3)
                dve.scalar_tensor_tensor(g_rows[g], g_tmp[0:B, 0, :], -1.0, g_tmp[0:B, 1, :],
                                         ALU.add, ALU.mult).then_inc(gate_rows, 1)

            def split_lo(w):
                dve.wait_ge(w_hi_done, w + 1)
                dve.scalar_tensor_tensor(W_lo[w].rearrange("p k n -> p (k n)"),
                                         w_stage[w].rearrange("p k n -> p (k n)"),
                                         QSCALE if w == 0 else 1.0,
                                         W_hi[w].bitcast(F32).rearrange("p k n -> p (k n)"),
                                         ALU.mult, ALU.subtract).then_inc(w_lo_done, 1)

            def proj_lo(b, pair, qk):
                dve.wait_ge(pj_hi, b * H + 2 * pair + qk + 1)
                for w, src, other in ((0, slice(0, D), slice(D, P)), (1, slice(D, P), slice(0, D))):
                    hi = (qs, kh)[qk][src, pair % 2, w, :].bitcast(F32)
                    dst = qs[other, pair % 2, w, :] if qk == 0 else kl[src, pair % 2, :]
                    d = dve.scalar_tensor_tensor(dst, PJ[src, :], bqkv[src, qk, pair:pair + 1], hi,
                                                 ALU.add, ALU.subtract)
                d.then_inc(pj_done, 1)

            def row_max(b, h, st):
                dve.wait_ge(s_ready, b * 32 + 4 * h + st + 1)
                dve.tensor_reduce(negmax[:, h % 2, st:st + 1], SC[st], AXX, ALU.max, negate=True)\
                    .then_inc(max_done, 1)

            def row_recips(b, h, st):
                dve.wait_ge(exp_done, b * 32 + 4 * h + st + 2)
                dve.reciprocal(rinv[:, h % 2, st:st + 2], ssum[:, h % 2, st:st + 2]).then_inc(rinv_done, 1)

            def weights_lo(b, h, j):
                dve.wait_ge(pt_hi_done, b * 32 + 4 * h + j + 1)
                dve.tensor_tensor(pt_lo[:, j, :], TB[turn_pos(h, j) % 2], pt_hi[:, j, :].bitcast(F32),
                                  ALU.subtract).then_inc(ring_free, 1)

            def join_halves(b, h):
                dve.wait_ge(c_done, b * H + h + 1)
                rows_ = slice(D * (h % 2), D * (h % 2) + D)
                dve.scalar_tensor_tensor(a32[rows_, h // 2 % 2, :], PVB[0:D, :], bv_h[:, h:h + 1], c32[:, :],
                                         ALU.add, ALU.add).then_inc(pv_free, 1)

            def result_hi(b, pair):
                dve.wait_ge(pv_free, b * H + 2 * pair + 3)
                dve.tensor_copy(a_hi[:, pair, :], a32[:, pair % 2, :]).then_inc(ahi_done, 1)

            def v_los(b, t, bank):
                dve.wait_ge(v_hi, b * ST + t + 1)
                dve.tensor_tensor(v_sb[:, t, :, 1, :], bank.rearrange("p (h d) -> p h d", d=D),
                                  v_sb[:, t, :, 0, :].bitcast(F32), ALU.subtract).then_inc(v_done, 1)

            def split_lo_b(m):
                dve.wait_ge(whi_done, m + 1)
                for j in range(3):
                    d = dve.scalar_tensor_tensor(w_ff[:, m, 2 * j + 1, :], w_raw[:, m % 2, j, :], -ZERO_POINT,
                                                 w_ff[:, m, 2 * j, :].bitcast(F32), ALU.add, ALU.subtract)
                d.then_inc(wlo_done, 1)

            dve.sem_inc(ring_free, 2)
            dve.sem_inc(pv_free, 1)
            dve.sem_inc(y_done, ST)
            mod_columns(SA, 1)
            split_lo(0)
            mod_columns(CA, 2)
            split_lo(1)
            for f in range(KT):
                norm_hi(0, f)
            proj_lo(0, 0, 0)
            split_lo(2)
            proj_lo(0, 0, 1)
            v_los(0, 0, TB[0])
            v_los(0, 1, TB[1])
            for st in range(ST):
                row_max(0, 0, st)
            row_recips(0, 0, 0)
            row_recips(0, 0, 2)
            proj_lo(0, 1, 0)
            dve.wait_ge(h_done, KT)
            gate(0, 3)
            v_los(0, 2, TB[0])
            split_lo(3)
            proj_lo(0, 1, 1)
            norm_tokens(1)
            mod_columns(SB, 4)
            mod_columns(CB, 5)
            gate(1, 6)
            v_los(0, 3, TB[1])
            dve.wait_ge(fs_loaded, 32)
            dve.scalar_tensor_tensor(sgu_half[:, :], sg_half[:, :], 0.5, su_col[:, :], ALU.mult, ALU.mult)\
                .then_inc(fs_step, 1)
            dve.wait_ge(fs_step, 1)
            dve.tensor_scalar(sg_half[:, :], sg_half[:, :], 0.5, None, ALU.mult).then_inc(fs_step, 1)

            def attention(b, later):
                more = later > 0
                for h in range(H):
                    norm = h == 4
                    after = (b, h + 1) if h < H - 1 else (b + 1, 0)
                    last = h == H - 1 and not more

                    def next_max(st):
                        if not last:
                            row_max(*after, st)

                    def next_recips(st):
                        if not last:
                            row_recips(*after, st)

                    def next_norm(f):
                        if norm:
                            norm_hi(b + 1, f)

                    if h and h != 5:
                        weights_lo(b, h - 1, 2)
                    next_max(0)
                    if h and h != 5:
                        weights_lo(b, h - 1, 3)
                    next_max(1)
                    next_norm(0)
                    if norm:
                        weights_lo(b, h, 0)
                        next_recips(0)
                        next_max(2)
                    else:
                        next_max(2)
                        next_recips(0)
                        weights_lo(b, h, 0)
                    next_norm(1)
                    if h:
                        join_halves(b, h - 1)
                    next_max(3)
                    if h and h % 2 == 0:
                        result_hi(b, h // 2 - 1)
                    weights_lo(b, h, 1)
                    next_recips(2)
                    if norm:
                        norm_hi(b + 1, 2)
                        weights_lo(b, h, 2)
                        norm_hi(b + 1, 3)
                        weights_lo(b, h, 3)
                    if h < 4 or more:
                        nxt, pair, qk = filler_of(h)
                        proj_lo(b + nxt, pair, qk)
                weights_lo(b, H - 1, 2)
                weights_lo(b, H - 1, 3)
                if more:
                    v_los(b + 1, 0, SC[0])
                join_halves(b, H - 1)
                result_hi(b, PAIRS - 1)
                for t in range(1, ST if more else 0):
                    if later:
                        norm_stats(b + 2, t - 1)
                    v_los(b + 1, t, SC[t])
                if later:
                    norm_stats(b + 2, ST - 1)
                    norm_aggr(b + 2)
                if not more:
                    split_lo_b(0)
                    split_lo_b(1)
                dve.wait_ge(gate_loaded, b * 16 + 16)
                for s in range(ST):
                    n = out_pos(s)
                    dve.wait_ge(ring_ready, ring(b, n))
                    dve.wait_ge(x_done, b * ST + s + 1)
                    dve.tensor_tensor(t32[:, s % 2, :], TB[n % 2], gate_bc[:, :], ALU.mult).then_inc(ring_free, 1)
                    if later:
                        norm_scale(b + 2, s)

            with dve.Fori(0, B - 2) as b:
                attention(b, 2)
            attention(B - 2, 1)
            attention(B - 1, 0)

            G = [psum[:, 0, :], psum[:, 2, :]]
            U = [psum[:, 1, :], psum[:, 3, :]]
            Y = [psum[:, 4 + s, :] for s in range(ST)]

            def ff_norm_part(b):
                for u, fs in enumerate(((0, 1), (2,), (3,))):
                    dve.wait_ge(unit_ready, b * UNITS + MT + u + 1)
                    if u:
                        dve.wait_ge(fh_done, b * KT + u)
                    for f in fs:
                        d = modulate(f, b + 1, 2, (G if f != 1 else U)[(MT + u) % 2])
                    d.then_inc(unit_free, 1)
                    for f in fs:
                        dve.wait_ge(fh_hi, b * KT + f + 1)
                        norm_lo(f).then_inc(fh_done, 1)

            def weights_flag():
                dve.wait_ge(squares_done, 3 * MT)
                dve.tensor_reduce(lo_sum[:, :], lo_sums[:, :], AXX, ALU.max).then_inc(lo_summed, 1)
                dve.wait_ge(lo_turned, 16)
                dve.tensor_reduce(lo_all[:, :], lo_row[:, :], AXX, ALU.max).then_inc(lo_summed, 1)
                dve.wait_ge(lo_summed, 2)
                dve.tensor_scalar(lo_flag[:, :], lo_all[:, :], 0.0, None, ALU.is_gt).then_inc(lo_known, 1)

            def feed_forward(b, bi, more):
                for m in range(MT):
                    if bi == 0 and 2 <= m + 1 < MT:
                        split_lo_b(m + 1)
                    u = m % 2
                    dve.wait_ge(tanh_done, b * MT + m + 1)
                    dve.scalar_tensor_tensor(a_sb[:, :], tanh_sb[:, :], 1.0, G[u], ALU.add, ALU.mult)\
                        .then_inc(a_step, 1)
                    dve.wait_ge(a_step, b * MT + m + 1)
                    dve.scalar_tensor_tensor(g32[:, :], U[u], sgu_half[:, m:m + 1], a_sb[:, :],
                                             ALU.mult, ALU.mult).then_inc(unit_free, 1)
                    dve.wait_ge(ghi_done, b * MT + m + 1)
                    dve.tensor_tensor(g_lo[:, m % 2, :], g32[:, :], g_hi[:, m % 2, :].bitcast(F32),
                                      ALU.subtract).then_inc(g_done, 1)
                    if m == 2 and more:
                        for t in range(ST):
                            norm_stats(b + B + 1, t)
                        norm_aggr(b + B + 1)
                    if m == 5 and more:
                        for t in range(ST):
                            norm_scale(b + B + 1, t)
                    if bi == 0 and m == MT - 1:
                        weights_flag()
                if more:
                    ff_norm_part(b)
                dve.wait_ge(gs_done, b + 1)
                dve.wait_ge(d_done, b * MT + MT)
                for s in range(ST):
                    dve.wait_ge(fx_done, b * ST + s + 1)
                    dve.tensor_tensor(t32[:, s % 2, :], Y[s], gate_bc[:, :], ALU.mult).then_inc(y_done, 1)

            feed_forward(0, 0, True)
            with dve.Fori(1, B - 1) as b:
                feed_forward(b, 1, True)
            feed_forward(B - 1, B - 1, False)

        @block.gpsimd
        def _(pool):
            pool.memset(ident[:, :], 0.0).then_inc(ln_step, 1)
            pool.memset(neg_half[:, :], -0.5).then_inc(ln_step, 1)
            pool.memset(ones_f[:, :], 1.0).then_inc(ln_step, 1)
            pool.memset(eps_t[:, :], EPS).then_inc(ln_step, 1)
            pool.memset(three_halves[:, :], 1.5).then_inc(ln_step, 1)
            pool.wait_ge(ln_step, 5)
            pool.affine_select(out=ident[:, :], in_=ident[:, :], compare_op=ALU.not_equal, fill=1.0, base=0,
                               pattern=[[-1, P]], channel_multiplier=1).then_inc(const_ready, 1)
            pool.sem_inc(x_done, 2)
            pool.sem_inc(fx_done, 2)

            def inv_std(b):
                def after(k):
                    pool.wait_ge(ln_step, b * 6 + 5 + k)

                pool.wait_ge(aggr_done, b * ST + ST)
                pool.tensor_tensor(veps[:, :], mv[:, :, 1], eps_t[:, :], ALU.add).then_inc(ln_step, 1)
                after(1)
                pool.tensor_tensor(rstd[:, :], veps[:, :], neg_half[:, :], ALU.pow).then_inc(ln_step, 1)
                after(2)
                pool.tensor_tensor(newt[:, :], rstd[:, :], rstd[:, :], ALU.mult).then_inc(ln_step, 1)
                after(3)
                pool.tensor_tensor(newt[:, :], newt[:, :], veps[:, :], ALU.mult).then_inc(ln_step, 1)
                after(4)
                pool.tensor_tensor(newt[:, :], newt[:, :], neg_half[:, :], ALU.mult).then_inc(ln_step, 1)
                after(5)
                pool.tensor_tensor(newt[:, :], newt[:, :], three_halves[:, :], ALU.add).then_inc(ln_step, 1)
                after(6)
                pool.tensor_tensor(rstd[:, :], rstd[:, :], newt[:, :], ALU.mult).then_inc(rstd_done, 1)

            def divide(b, h, st):
                if st % 2 == 0:
                    pool.wait_ge(rinv_done, b * 16 + 2 * h + st // 2 + 1)
                row = pr[:, h % 2, st, :]
                pool.tensor_tensor(row, row, rinv[:, h % 2, st:st + 1].to_broadcast([P, S]), ALU.mult)\
                    .then_inc(p_done, 1)

            def norm_lo(b, f):
                pool.wait_ge(h_hi, b * KT + f + 1)
                pool.tensor_tensor(hT_lo[:, f, :], h32[:, f % 2, :], hT_hi[:, f, :].bitcast(F32),
                                   ALU.subtract).then_inc(h_done, 1)

            def result_lo(b, pair):
                pool.wait_ge(ahi_done, b * PAIRS + pair + 1)
                pool.tensor_tensor(a_lo[:, pair, :], a32[:, pair % 2, :], a_hi[:, pair, :].bitcast(F32),
                                   ALU.subtract).then_inc(a_done, 1)

            inv_std(0)
            for f in range(KT):
                norm_lo(0, f)
            for st in range(ST):
                divide(0, 0, st)
            inv_std(1)

            def attention(b, later):
                more = later > 0
                for h in range(H):
                    after = (b, h + 1) if h < H - 1 else (b + 1, 0)
                    for st in range(0 if h == H - 1 and not more else ST):
                        divide(*after, st)
                        if h == 4 and st:
                            for f in ((0, 1), (2,), (3,))[st - 1]:
                                norm_lo(b + 1, f)
                    if h and h % 2 == 0:
                        result_lo(b, h // 2 - 1)
                result_lo(b, PAIRS - 1)
                if later:
                    inv_std(b + 2)
                pool.wait_ge(xr_loaded, b * 16 + 16)
                for s in range(ST):
                    pool.wait_ge(ring_free, ring(b, out_pos(s)) + 2)
                    pool.tensor_tensor(xr[:, s, :], xr[:, s, :], t32[:, s % 2, :], ALU.add).then_inc(x_done, 1)

            with pool.Fori(0, B - 2) as b:
                attention(b, 2)
            attention(B - 2, 1)
            attention(B - 1, 0)

            pool.wait_ge(sdown_loaded, 16)

            def feed_forward(b, more):
                pool.wait_ge(fg_loaded, b * 16 + 16)
                pool.tensor_tensor(gate_bc[:, :], gate_bc[:, :], sdown_bc[:, :], ALU.mult).then_inc(gs_done, 1)
                if more:
                    inv_std(b + B + 1)
                pool.wait_ge(fr_loaded, b * 16 + 16)
                for s in range(ST):
                    pool.wait_ge(y_done, b * ST + ST + s + 1)
                    pool.tensor_tensor(xr[:, s, :], xr[:, s, :], t32[:, s % 2, :], ALU.add).then_inc(fx_done, 1)

            with pool.Fori(0, B - 1) as b:
                feed_forward(b, True)
            feed_forward(B - 1, False)


def kernel(L0_attn_x, L0_attn_Wq, L0_attn_bq, L0_attn_Wk, L0_attn_bk, L0_attn_Wv, L0_attn_bv, L0_attn_Wo,
           L0_attn_bo, L0_ffn_wq_gate, L0_ffn_s_gate, L0_ffn_wq_up, L0_ffn_s_up, L0_ffn_wq_down, L0_ffn_s_down,
           L0_c, L0_wmod):
    import numpy as np
    import concourse.bacc as bacc
    from concourse.bass_utils import run_bass_kernel_spmd

    def tiles_in(w):
        return np.asarray(w).reshape(MT, P, KT, P).transpose(0, 3, 2, 1).reshape(MT, P, F)

    arrays = {
        "x": L0_attn_x,
        "c_t": np.asarray(L0_c).T,
        "wmod": L0_wmod,
        "w_q": L0_attn_Wq, "w_k": L0_attn_Wk, "w_v": L0_attn_Wv, "w_o": L0_attn_Wo,
        "b_q": np.asarray(L0_attn_bq).reshape(PAIRS, P).T,
        "b_k": np.asarray(L0_attn_bk).reshape(PAIRS, P).T,
        "b_v": np.asarray(L0_attn_bv).reshape(H, D).T,
        "b_o": np.asarray(L0_attn_bo).reshape(1, F),
        "w_gate": tiles_in(L0_ffn_wq_gate),
        "w_up": tiles_in(L0_ffn_wq_up),
        "w_down": np.asarray(L0_ffn_wq_down).reshape(F, MT, P).transpose(1, 2, 0),
        "s_gate": np.asarray(L0_ffn_s_gate).reshape(MT, P).T,
        "s_up": np.asarray(L0_ffn_s_up).reshape(MT, P).T,
        "s_down": np.asarray(L0_ffn_s_down).reshape(1, F),
    }
    arrays = {n: np.ascontiguousarray(a) for n, a in arrays.items()}
    nc = bacc.Bacc("TRN2", target_bir_lowering=False, num_devices=1)
    args = {n: nc.dram_tensor(n, a.shape, mybir.dt.from_np(a.dtype), kind="ExternalInput").ap()
            for n, a in arrays.items()}
    out = nc.dram_tensor("out", (B, S, F), F32, kind="ExternalOutput").ap()
    adaln_block(nc, **args, out=out)
    r = run_bass_kernel_spmd(nc, [arrays], core_ids=[0])
    return r.results[0]["out"]
```

```python
from contextlib import ExitStack

import concourse.bass as bass
from concourse import mybir

F32 = mybir.dt.float32
R32 = mybir.dt.float32r
I32 = mybir.dt.int32
ALU = mybir.AluOpType
ACT = mybir.ActivationFunctionType
AXX = mybir.AxisListType.X

P = 128
B, S, F = 8, 512, 512
H, D = 8, 64
HID = 1408
KT = F // P
ST = S // P
PAIRS = H // 2
MT = HID // P
ZERO_POINT = 128.0
EPS = 1e-5
QSCALE = 8.0 ** -0.5
SA, CA, GA, SB, CB, GB = range(6)

RING = H * ST + ST


def turn_pos(h, j):
    return ST * h + j


def out_pos(s):
    return H * ST + s


def filler_of(h):
    if h < 4:
        return 0, 2 + h // 2, h % 2
    return 1, (h - 4) // 2, h % 2


def adaln_block(nc, x, c_t, wmod, w_q, w_k, w_v, w_o, b_q, b_k, b_v, b_o, w_gate, w_up, w_down,
                s_gate, s_up, s_down, out):
    x1_dram = nc.dram_tensor("x1_scratch", [B, S, F], F32, kind="Internal").ap()
    gates_dram = nc.dram_tensor("gates_scratch", [2, B, F], F32, kind="Internal").ap()

    def tokens(a, b):
        return a[b, :, :].rearrange("(t p) f -> p t f", p=P)

    with ExitStack() as ctx:
        at = [0]
        place_of = {}

        def sb(name, shape, dt=F32):
            n = 4
            for d in shape[1:]:
                n *= d
            t = nc.alloc_sbuf_tensor_at(name, shape, dt, offset=at[0])
            place_of[t.name] = at[0]
            at[0] += (n + 31) // 32 * 32
            assert at[0] <= TOP, (name, at[0], TOP)
            return t

        at[0] = (nc.sbuf_base + 31) // 32 * 32
        TOP = at[0] + nc.sbuf_bytes_remaining // 32 * 32 - 32

        def as_f32(t, name, shape):
            return nc.alloc_sbuf_tensor_at(name, shape, F32, offset=place_of[t.name])

        def sem(name):
            return ctx.enter_context(nc.semaphore(name))

        ident = sb("ident", [P, P])
        modc = sb("modc", [P, 4, KT, B])
        neg_half = sb("neg_half", [P, ST])
        three_halves = sb("three_halves", [P, ST])
        eps_t = sb("eps_t", [P, ST])
        stats = sb("stats", [P, ST, 6])
        mv = sb("mv", [P, ST, 2])
        veps = sb("veps", [P, ST])
        rstd = sb("rstd", [P, ST])
        newt = sb("newt", [P, ST])
        h32 = sb("h32", [P, 2, S])
        xn = sb("xn", [P, ST, F])
        xr = sb("xr", [P, ST, F])
        hT_hi = sb("hT_hi", [P, KT, S], R32)
        hT_lo = sb("hT_lo", [P, KT, S], R32)
        gate_bc = sb("gate_bc", [P, F])
        t32 = sb("t32", [P, 2, F])
        sg_half = sb("sg_half", [P, MT])
        su_col = sb("su_col", [P, MT])
        sgu_half = sb("sgu_half", [P, MT])
        both = at[0]
        Wp_hi = sb("Wp_hi", [P, 3, KT, F], R32)
        Wp_lo = sb("Wp_lo", [P, 3, KT, F], R32)
        projections_end = at[0]
        bqkv = sb("bqkv", [P, 3, PAIRS])
        bv_h = sb("bv_h", [D, H])
        c_sb = sb("c_sb", [P, KT, B])
        c_th = sb("c_th", [P, KT, B])
        c_silu = sb("c_silu", [P, KT, B])
        negmax = sb("negmax", [P, 2, ST])
        ssum = sb("ssum", [P, 2, ST])
        rinv = sb("rinv", [P, 2, ST])
        bo_hi = sb("bo_hi", [1, F], R32)
        bo_lo = sb("bo_lo", [1, F], R32)
        ones_f = sb("ones_f", [1, P])
        ones_r = sb("ones_r", [1, P], R32)
        Wo_hi = sb("Wo_hi", [P, KT, F], R32)
        Wo_lo = sb("Wo_lo", [P, KT, F], R32)
        W_hi = [Wp_hi[:, i, :, :] for i in range(3)] + [Wo_hi[:, :, :]]
        W_lo = [Wp_lo[:, i, :, :] for i in range(3)] + [Wo_lo[:, :, :]]
        qs = sb("qs", [P, 2, 2, S], R32)
        kh = sb("kh", [P, 2, 2, S], R32)
        kl = sb("kl", [P, 2, S], R32)
        v_sb = sb("v_sb", [P, ST, H, 2, D], R32)
        pr = sb("pr", [P, 2, ST, S])
        pt_hi = sb("pt_hi", [P, ST, S], R32)
        pt_lo = sb("pt_lo", [P, ST, S], R32)
        c32 = sb("c32", [D, S])
        a32 = sb("a32", [P, 2, S])
        bo_f = h32[0:1, 0, :]
        a_hi = sb("a_hi", [P, PAIRS, S], R32)
        a_lo = sb("a_lo", [P, PAIRS, S], R32)
        g_tmp = t32
        g_rows = [h32[0:B, g, :] for g in range(2)]
        pt_hi_f = as_f32(pt_hi, "pt_hi_f", [P, ST, S])
        pt_lo_f = as_f32(pt_lo, "pt_lo_f", [P, ST, S])
        a_hi_f = as_f32(a_hi, "a_hi_f", [P, PAIRS, S])
        a_lo_f = as_f32(a_lo, "a_lo_f", [P, PAIRS, S])
        at[0] = both
        w_raw = sb("w_raw", [P, 2, 3, F], I32)
        EARLY = (projections_end - at[0]) // (6 * F * 4)
        assert EARLY >= 2
        w_ff = sb("w_ff", [P, MT, 6, F], R32)
        g_hi = sb("g_hi", [P, 2, S], R32)
        g_lo = sb("g_lo", [P, 2, S], R32)
        tanh_sb = sb("tanh_sb", [P, S])
        a_sb = sb("a_sb", [P, S])
        g32 = sb("g32", [P, S])
        lo_square = sb("lo_square", [P, F])
        lo_sums = sb("lo_sums", [P, 3 * MT])
        lo_sum = sb("lo_sum", [P, 1])
        lo_row = sb("lo_row", [1, P])
        lo_all = sb("lo_all", [1, 1])
        lo_flag = sb("lo_flag", [1, 1], I32)
        sdown_bc = sb("sdown_bc", [P, F])

        psum = nc.alloc_psum_tensor("banks", [P, 8, 512], F32)
        SC = [psum[:, i, :] for i in range(4)]
        TB = [psum[:, 4 + i, :] for i in range(2)]
        PVB = psum[:, 6, :]
        PJ = psum[:, 7, :]

        const_ready = sem("const_ready")
        small_loaded = sem("small_loaded")
        c_loaded = sem("c_loaded")
        wmod_loaded = [sem(f"wmod{n}_loaded") for n in range(6)]
        w_loaded = [sem(f"w_{c}_loaded") for c in "qkvo"]
        silu_step = sem("silu_step")
        bias_ready = sem("bias_ready")
        mod_mm = sem("mod_mm")
        mod_col = sem("mod_col")
        gate_step = sem("gate_step")
        gate_rows = sem("gate_rows")
        gates_stored = sem("gates_stored")
        w_hi_done = sem("w_hi_done")
        w_lo_done = sem("w_lo_done")
        xn_loaded = sem("xn_loaded")
        xr_loaded = sem("xr_loaded")
        gate_loaded = sem("gate_loaded")
        bn_done = sem("bn_done")
        aggr_begun = sem("aggr_begun")
        aggr_done = sem("aggr_done")
        ln_step = sem("ln_step")
        rstd_done = sem("rstd_done")
        ln_done = sem("ln_done")
        ring_ready = sem("ring_ready")
        ring_free = sem("ring_free")
        pj_ready = sem("pj_ready")
        pj_hi = sem("pj_hi")
        pj_done = sem("pj_done")
        h32_done = sem("h32_done")
        h_hi = sem("h_hi")
        h_done = sem("h_done")
        k_copied = sem("k_copied")
        norm_turned = sem("norm_turned")
        v_ready = sem("v_ready")
        v_hi = sem("v_hi")
        v_done = sem("v_done")
        s_ready = sem("s_ready")
        max_done = sem("max_done")
        exp_done = sem("exp_done")
        rinv_done = sem("rinv_done")
        p_done = sem("p_done")
        pt_hi_done = sem("pt_hi_done")
        pv_ready = sem("pv_ready")
        c_done = sem("c_done")
        pv_free = sem("pv_free")
        ahi_done = sem("ahi_done")
        a_done = sem("a_done")
        x_done = sem("x_done")
        x1_stored = sem("x1_stored")
        fs_loaded = sem("fs_loaded")
        fs_step = sem("fs_step")
        wraw_loaded = [sem(f"wraw{i}_loaded") for i in range(2)]
        sdown_loaded = sem("sdown_loaded")
        whi_done = sem("whi_done")
        wlo_done = sem("wlo_done")
        squares_done = sem("squares_done")
        lo_summed = sem("lo_summed")
        lo_turned = sem("lo_turned")
        lo_known = sem("lo_known")
        fr_loaded = sem("fr_loaded")
        fg_loaded = sem("fg_loaded")
        unit_ready = sem("unit_ready")
        unit_free = sem("unit_free")
        fn_turned = sem("fn_turned")
        f32_done = sem("f32_done")
        fh_hi01 = sem("fh_hi01")
        fh_hi23 = sem("fh_hi23")
        fh_done01 = sem("fh_done01")
        fh_done23 = sem("fh_done23")
        tanh_done = sem("tanh_done")
        a_step = sem("a_step")
        ghi_done = sem("ghi_done")
        g_done = sem("g_done")
        d_done = sem("d_done")
        gs_done = sem("gs_done")
        y_done = sem("y_done")
        fx_done = sem("fx_done")
        stored = sem("stored")

        block = ctx.enter_context(nc.Block())

        def ring(b, pos):
            return b * RING + pos + 1

        def pair_of(m):
            return m % 2 if m < MT - 1 else 1 - m % 2

        w_stage = [pt_hi_f[:, :, :], pt_lo_f[:, :, :], xr[:, :, :], a_hi_f[:, :, :]]
        wmod_stage = [pr[:, 0, :, :], pr[:, 1, :, :], a_lo_f[:, :, :], pt_hi_f[:, :, :], pt_lo_f[:, :, :],
                      pr[:, 1, :, :]]
        COLS = {SA: 0, CA: 1, SB: 2, CB: 3}

        @block.sync
        def _(sp):
            def load_w(n):
                sp.dma_start(w_stage[n], (w_q, w_k, w_v, w_o)[n].rearrange("(k p) n -> p k n", p=P))\
                    .then_inc(w_loaded[n], 16)

            def load_wmod(n):
                sp.dma_start(wmod_stage[n], wmod[:, n * F:(n + 1) * F].rearrange("(k p) n -> p k n", p=P))\
                    .then_inc(wmod_loaded[n], 16)

            sp.dma_start(c_sb[:, :, :], c_t.rearrange("(k p) b -> p k b", p=P)).then_inc(c_loaded, 16)
            load_wmod(SA)
            sp.dma_start(xn[:, :, :], tokens(x, 0)).then_inc(xn_loaded, 16)
            load_wmod(CA)
            for j, bias in enumerate((b_q, b_k)):
                sp.dma_start(bqkv[:, j, :], bias).then_inc(small_loaded, 16)
            sp.dma_start(bv_h[:, :], b_v).then_inc(small_loaded, 16)
            sp.dma_start(bo_f, b_o).then_inc(small_loaded, 16)
            load_w(0)
            load_w(1)
            load_w(2)
            load_wmod(GA)
            load_w(3)

            def stores(b):
                for s in range(ST):
                    sp.wait_ge(x_done, b * ST + s + 3)
                    sp.dma_start(x1_dram[b, s * P:(s + 1) * P, :], xr[:, s, :]).then_inc(x1_stored, 16)

            def load_xn(i, src, b):
                sp.wait_ge(norm_turned, i * KT)
                sp.dma_start(xn[:, :, :], tokens(src, b)).then_inc(xn_loaded, 16)

            def attention(b, later):
                if later == 2:
                    load_xn(b + 2, x, b + 2)
                elif later == 1:
                    load_xn(B, x1_dram, 0)
                if not later:
                    sp.wait_ge(pj_ready, B * H)
                    ff_tile(0)
                    ff_tile(1)
                    load_xn(B + 1, x1_dram, 1)
                stores(b)
                if later:
                    sp.wait_ge(x1_stored, b * 64 + 64)
                    sp.dma_start(xr[:, :, :], tokens(x, b + 1)).then_inc(xr_loaded, 16)
                    sp.dma_start(gate_bc[:, :], gates_dram[0, bass.ds(b + 1, 1), :].partition_broadcast(P))\
                        .then_inc(gate_loaded, 16)

            def ff_tile(m):
                for j, w in enumerate((w_gate, w_up, w_down)):
                    sp.dma_start(w_raw[:, m % 2, j, :], w[m, :, :]).then_inc(wraw_loaded[m % 2], 16)

            sp.dma_start(sg_half[:, :], s_gate).then_inc(fs_loaded, 16)
            sp.dma_start(su_col[:, :], s_up).then_inc(fs_loaded, 16)
            sp.wait_ge(w_lo_done, 1)
            load_wmod(SB)
            sp.wait_ge(mod_mm, 2)
            load_wmod(GB)
            sp.wait_ge(w_lo_done, 2)
            load_wmod(CB)
            load_xn(1, x, 1)
            sp.wait_ge(w_lo_done, 3)
            sp.dma_start(xr[:, :, :], tokens(x, 0)).then_inc(xr_loaded, 16)
            for g in range(2):
                sp.wait_ge(gate_rows, g + 1)
                sp.dma_start(gates_dram[g, :, :], g_rows[g]).then_inc(gates_stored, 16)
            sp.wait_ge(gates_stored, 32)
            sp.dma_start(gate_bc[:, :], gates_dram[0, 0:1, :].partition_broadcast(P)).then_inc(gate_loaded, 16)
            with sp.Fori(0, B - 2) as b:
                attention(b, 2)
            attention(B - 2, 1)
            attention(B - 1, 0)
            sp.wait_ge(wlo_done, 1)
            ff_tile(2)
            sp.wait_ge(x1_stored, B * 64)

            sp.dma_start(xr[:, :, :], tokens(x1_dram, 0)).then_inc(fr_loaded, 16)
            sp.dma_start(gate_bc[:, :], gates_dram[1, 0:1, :].partition_broadcast(P)).then_inc(fg_loaded, 16)
            for m in range(3, MT):
                sp.wait_ge(wlo_done, m - 1)
                ff_tile(m)
                if m == 3:
                    sp.dma_start(sdown_bc[:, :], s_down.partition_broadcast(P)).then_inc(sdown_loaded, 16)
            sp.wait_ge(lo_summed, 1)
            sp.dma_start(lo_row[0:1, :], lo_sum[:, :]).then_inc(lo_turned, 16)

            def out_stores(b):
                for s in range(ST):
                    sp.wait_ge(fx_done, b * ST + s + 3)
                    sp.dma_start(out[b, s * P:(s + 1) * P, :], xr[:, s, :]).then_inc(stored, 16)

            def turn_over(b):
                out_stores(b)
                sp.wait_ge(stored, b * 64 + 64)
                sp.dma_start(xr[:, :, :], tokens(x1_dram, b + 1)).then_inc(fr_loaded, 16)
                sp.dma_start(gate_bc[:, :], gates_dram[1, bass.ds(b + 1, 1), :].partition_broadcast(P))\
                    .then_inc(fg_loaded, 16)

            turn_over(0)
            with sp.Fori(1, B - 1) as b:
                sp.wait_ge(fn_turned, b * 3)
                sp.dma_start(xn[:, :, :], tokens(x1_dram, b + 1)).then_inc(xn_loaded, 16)
                turn_over(b)
            out_stores(B - 1)
            sp.wait_ge(stored, B * 64)

        @block.tensor
        def _(pe):
            def turn_norm(f, bank):
                for t in range(ST):
                    mm = pe.transpose(bank[:, t * P:(t + 1) * P], xn[:, t, f * P:(f + 1) * P], ident[:, :])
                return mm

            def project(bank, w, m, steps=range(12), ready=None):
                for i in steps:
                    k, part = divmod(i, 3)
                    if part == 0 and ready is not None:
                        ready(k)
                    lhs = (W_lo if part == 2 else W_hi)[w][:, k, m * P:(m + 1) * P]
                    rhs = (hT_lo if part == 1 else hT_hi)[:, k, :]
                    mm = pe.matmul(bank, lhs, rhs, start=(i == 0), stop=(i == 11))
                return mm

            def scores(b, h, sts, first=False):
                pb, w = h // 2 % 2, h % 2
                if h == 1 and sts[0] == 0:
                    pe.wait_ge(v_done, b * ST + ST)
                if sts[0] == 0:
                    pe.wait_ge(pj_done, b * H + 2 * (h // 2) + 2)
                    pe.wait_ge(k_copied, b * PAIRS + h // 2 + 1)
                lo = slice(0, D) if w == 0 else slice(D, P)
                for st in sts:
                    if not first:
                        pe.wait_ge(exp_done, b * 32 + 4 * h + st - 3)
                    cols = slice(st * P, (st + 1) * P)
                    pe.matmul(SC[st], qs[:, pb, w, cols], kh[:, pb, w, :], start=True, stop=False)
                    pe.matmul(SC[st], qs[lo, pb, w, cols], kl[lo, pb, :], start=False, stop=True)\
                        .then_inc(s_ready, 1)

            def turn(b, h, j):
                n = turn_pos(h, j)
                pe.wait_ge(ring_free, ring(b, n))
                if j == 0:
                    pe.wait_ge(p_done, b * 32 + 4 * h + 4)
                for st in range(ST):
                    mm = pe.transpose(TB[n % 2][:, st * P:(st + 1) * P],
                                      pr[:, h % 2, st, j * P:(j + 1) * P], ident[:, :])
                mm.then_inc(ring_ready, 1)

            def pv(b, h, j):
                if j == 0:
                    pe.wait_ge(pv_free, b * H + h + 1)
                pe.wait_ge(ring_free, ring(b, turn_pos(h, j)) + 2)
                lhs = v_sb[:, j, h, :, :].rearrange("p a d -> p (a d)")
                pe.matmul(PVB, lhs, pt_hi[:, j, :], start=(j == 0), stop=False)
                mm = pe.matmul(PVB, lhs, pt_lo[:, j, :], start=False, stop=(j == ST - 1))
                if j == ST - 1:
                    mm.then_inc(pv_ready, 1)

            def values(t, bank):
                for i in range(12):
                    k, part = divmod(i, 3)
                    lhs = (hT_lo if part == 1 else hT_hi)[:, k, t * P:(t + 1) * P]
                    rhs = (W_lo if part == 2 else W_hi)[2][:, k, :]
                    mm = pe.matmul(bank, lhs, rhs, start=(i == 0), stop=(i == 11))
                return mm

            def output(s, bank):
                pe.matmul(bank, ones_r[:, :], bo_hi[:, :], start=True, stop=False)
                pe.matmul(bank, ones_r[:, :], bo_lo[:, :], start=False, stop=False)
                for i in range(12):
                    k, part = divmod(i, 3)
                    lhs = (a_lo if part == 1 else a_hi)[:, k, s * P:(s + 1) * P]
                    rhs = (W_lo if part == 2 else W_hi)[3][:, k, :]
                    mm = pe.matmul(bank, lhs, rhs, start=False, stop=(i == 11))
                return mm

            def mod_columns(kind):
                pe.wait_ge(wmod_loaded[kind], 16)
                bank = SC[COLS[kind]]
                for f in range(KT):
                    for k in range(KT):
                        mm = pe.matmul(bank[:, f * B:(f + 1) * B], wmod_stage[kind][:, k, f * P:(f + 1) * P],
                                       c_silu[:, k, :], start=(k == 0), stop=(k == KT - 1))
                mm.then_inc(mod_mm, 1)

            def mod_rows(kind):
                pe.wait_ge(wmod_loaded[kind], 16)
                for k in range(KT):
                    mm = pe.matmul(PVB[0:B, :], c_silu[:, k, :], wmod_stage[kind][:, k, :],
                                   start=(k == 0), stop=(k == KT - 1))
                mm.then_inc(mod_mm, 1)

            def first_projection(i):
                if i:
                    pe.wait_ge(pj_done, i)
                if i < 2:
                    pe.wait_ge(w_lo_done, i + 1)
                project(PJ, i % 2, i // 2, ready=lambda k: pe.wait_ge(h_done, k + 1)).then_inc(pj_ready, 1)

            def first_values(t):
                if t == 0:
                    pe.wait_ge(w_lo_done, 3)
                if t >= 2:
                    pe.wait_ge(v_done, t - 1)
                values(t, TB[t % 2]).then_inc(v_ready, 1)

            pe.wait_ge(silu_step, 3)
            mod_columns(SA)
            mod_columns(CA)
            pe.wait_ge(const_ready, 1)
            for f in range(KT):
                if f == 0:
                    pe.wait_ge(ln_done, ST)
                if f >= 2:
                    pe.wait_ge(h32_done, f - 1)
                turn_norm(f, TB[f % 2]).then_inc(norm_turned, 1)
            first_projection(0)
            first_values(0)
            first_projection(1)
            first_values(1)
            scores(0, 0, range(ST), first=True)
            first_projection(2)
            mod_rows(GA)
            first_values(2)
            first_projection(3)
            pe.wait_ge(exp_done, ST)
            mod_columns(SB)
            mod_columns(CB)
            pe.wait_ge(gate_rows, 1)
            mod_rows(GB)
            first_values(3)
            pe.wait_ge(mod_col, 4)
            pe.wait_ge(gate_rows, 2)
            pe.wait_ge(w_lo_done, 4)

            def filler(b, h, steps):
                nxt, pair, qk = filler_of(h)
                bb = b + nxt
                use = bb * H + 2 * pair + qk
                if steps[0] == 0:
                    pe.wait_ge(pj_done, use)
                mm = project(PJ, qk, pair, steps,
                             ready=(lambda k: pe.wait_ge(h_done, b * KT + KT + k + 1)) if h == 4 else None)
                if steps[-1] == 11:
                    mm.then_inc(pj_ready, 1)

            pe.wait_ge(v_done, ST)

            def norm_turn(b, f):
                if f == 0:
                    pe.wait_ge(ln_done, b * ST + 2 * ST)
                    pe.wait_ge(pj_done, b * H + 8)
                else:
                    pe.wait_ge(h32_done, b * KT + KT + f)
                turn_norm(f, PJ).then_inc(norm_turned, 1)

            def slot(b, h, more):
                after = (b, h + 1) if h < H - 1 else (b + 1, 0)
                last = h == H - 1 and not more
                fill = h < 4 or more
                if not last:
                    scores(*after, range(0, 3))
                if h:
                    pv(b, h - 1, 0)
                    pv(b, h - 1, 1)
                if not last:
                    scores(*after, range(3, 4))
                turn(b, h, 0)
                turn(b, h, 1)
                if fill:
                    filler(b, h, range(0, 8))
                if h:
                    pv(b, h - 1, 2)
                    pv(b, h - 1, 3)
                if fill:
                    filler(b, h, range(8, 10))
                turn(b, h, 2)
                if fill:
                    filler(b, h, range(10, 12))
                turn(b, h, 3)

            def norm_slot(b, h, more):
                after = (b, h + 1)
                scores(*after, range(0, 4))
                pv(b, h - 1, 0)
                turn(b, h, 0)
                norm_turn(b, 0)
                pv(b, h - 1, 1)
                turn(b, h, 1)
                norm_turn(b, 1)
                pv(b, h - 1, 2)
                turn(b, h, 2)
                norm_turn(b, 2)
                pv(b, h - 1, 3)
                turn(b, h, 3)
                norm_turn(b, 3)
                if more:
                    pe.wait_ge(h32_done, b * KT + 2 * KT)
                    filler(b, h, range(0, 12))

            def attention(b, more):
                for h in range(H):
                    (norm_slot if h == 4 else slot)(b, h, more)
                def next_values(t):
                    pe.wait_ge(exp_done, b * 32 + 32 + t + 1)
                    values(t, SC[t]).then_inc(v_ready, 1)

                if more:
                    next_values(0)
                for j in range(ST):
                    pv(b, H - 1, j)
                for t in range(1, ST if more else 0):
                    next_values(t)
                for s in range(ST):
                    n = out_pos(s)
                    pe.wait_ge(ring_free, ring(b, n))
                    if s == 0:
                        pe.wait_ge(a_done, b * PAIRS + PAIRS)
                    output(s, TB[n % 2]).then_inc(ring_ready, 1)

            with pe.Fori(0, B - 1) as b:
                attention(b, True)
            attention(B - 1, False)

            G = [psum[:, 0, :], psum[:, 2, :]]
            U = [psum[:, 1, :], psum[:, 3, :]]
            Y = [psum[:, 4 + s, :] for s in range(ST)]
            def ff_norm(b, f, bank):
                for t in range(ST):
                    mm = pe.transpose(bank[:, t * P:(t + 1) * P], xn[:, t, f * P:(f + 1) * P], ident[:, :])
                return mm

            def gate_up(b, m, bi, parts):
                u = pair_of(m)
                if m < 2:
                    if bi:
                        pe.wait_ge(f32_done, b * KT - KT + 3 + m)
                else:
                    pe.wait_ge(unit_free, b * MT + (m - 1 if m < MT - 1 else m))
                if bi == 0:
                    pe.wait_ge(wlo_done, m + 1)
                for j, bank in ((0, G[u]), (2, U[u])):
                    for i in range(KT * parts):
                        k, part = divmod(i, parts)
                        if m == 0 and part == 0 and bank is G[u]:
                            if bi == 0:
                                pe.wait_ge(h_done, B * KT + k + 1)
                            else:
                                pe.wait_ge(fh_done01 if k < 2 else fh_done23, b * 2 - 2 + k % 2 + 1)
                        mm = pe.matmul(bank, w_ff[:, m, j + part // 2, k * P:(k + 1) * P],
                                       (hT_lo if part == 1 else hT_hi)[:, k, :],
                                       start=(i == 0), stop=(i == KT * parts - 1))
                mm.then_inc(unit_ready, 1)

            def down(b, m, bi, parts):
                pe.wait_ge(g_done, b * MT + m + 1)
                for s in range(ST):
                    if m == 0:
                        if s == 0 and bi == 0:
                            pe.wait_ge(ring_free, ring(B - 1, out_pos(ST - 1)) + 2)
                        pe.wait_ge(y_done, b * ST + s + 1)
                    cols = slice(s * P, (s + 1) * P)
                    pe.matmul(Y[s], g_hi[:, m % 2, cols], w_ff[:, m, 4, :], start=(m == 0), stop=False)
                    last = m == MT - 1
                    mm = pe.matmul(Y[s], g_lo[:, m % 2, cols], w_ff[:, m, 4, :], start=False,
                                   stop=last and parts == 2)
                    if parts == 3:
                        mm = pe.matmul(Y[s], g_hi[:, m % 2, cols], w_ff[:, m, 5, :], start=False, stop=last)
                mm.then_inc(d_done, 1)

            def feed_forward(b, bi, more, parts):
                for m in range(MT):
                    if m == MT - 1 and more:
                        pe.wait_ge(ln_done, (b + B + 1) * ST + ST)
                        pe.wait_ge(unit_free, b * MT + MT - 2)
                        ff_norm(b, 0, G[0])
                        ff_norm(b, 1, U[0]).then_inc(fn_turned, 1)
                    gate_up(b, m, bi, parts)
                    if m:
                        down(b, m - 1, bi, parts)
                if more:
                    pe.wait_ge(f32_done, b * KT + 2)
                    ff_norm(b, 2, G[0]).then_inc(fn_turned, 1)
                    pe.wait_ge(unit_free, b * MT + MT)
                    ff_norm(b, 3, G[1]).then_inc(fn_turned, 1)
                down(b, MT - 1, bi, parts)

            feed_forward(0, 0, True, 3)

            def other_batches(parts):
                with pe.Fori(1, B - 1) as b:
                    feed_forward(b, 1, True, parts)
                feed_forward(B - 1, B - 1, False, parts)

            pe.wait_ge(lo_known, 1)
            with pe.If(pe.value_load(lo_flag[0:1, 0:1]) != 0):
                other_batches(3)
            with pe.Else():
                other_batches(2)
            pe.end_ifs()

        @block.scalar
        def _(act):
            act.wait_ge(c_loaded, 16)
            act.activation(c_th[:, :, :], c_sb[:, :, :], ACT.Tanh, scale=0.5).then_inc(silu_step, 1)
            act.wait_ge(small_loaded, 16 * 4)
            act.mul(bqkv[:, 0, :], bqkv[:, 0, :], QSCALE).then_inc(bias_ready, 1)
            act.activation(bo_hi[:, :], bo_f, ACT.Copy).then_inc(bias_ready, 1)

            def split_hi(w):
                act.wait_ge(w_loaded[w], 16)
                act.activation(W_hi[w], w_stage[w], ACT.Copy,
                               scale=QSCALE if w == 0 else 1.0).then_inc(w_hi_done, 1)

            def modulate(b, f, bank, kind=0, col=None):
                col = b if col is None else col
                act.wait_ge(norm_turned, b * KT + f + 1)
                if not (isinstance(b, int) and b == 0):
                    if f == 0:
                        act.wait_ge(gates_stored, 32)
                if not (isinstance(b, int) and b == 0 and f < 2):
                    act.wait_ge(h_done, b * KT + f - 1)
                act.activation(h32[:, f % 2, :], bank, ACT.Identity, bias=modc[:, kind, f, bass.ds(col, 1)],
                               scale=modc[:, kind + 1, f, bass.ds(col, 1)]).then_inc(h32_done, 1)

            def proj_hi(b, pair, qk):
                act.wait_ge(pj_ready, b * H + 2 * pair + qk + 1)
                for w, src in ((0, slice(0, D)), (1, slice(D, P))):
                    a = act.activation((qs, kh)[qk][src, pair % 2, w, :], PJ[src, :], ACT.Identity,
                                       bias=bqkv[src, qk, pair:pair + 1], scale=1.0)
                a.then_inc(pj_hi, 1)

            def k_copy(b, pair):
                act.wait_ge(pj_hi, b * H + 2 * pair + 2)
                for w, src, dst in ((0, slice(0, D), slice(D, P)), (1, slice(D, P), slice(0, D))):
                    a = act.activation(kh[dst, pair % 2, w, :], kh[src, pair % 2, w, :].bitcast(F32), ACT.Copy)
                a.then_inc(k_copied, 1)

            def exps(b, h, st):
                if st % 2 == 0:
                    act.wait_ge(max_done, b * 16 + 2 * h + st // 2 + 1)
                act.activation(pr[:, h % 2, st, :], SC[st], ACT.Exp, bias=negmax[:, h % 2, st:st + 1],
                               scale=1.0, accum_out=ssum[:, h % 2, st:st + 1]).then_inc(exp_done, 1)

            def weights_hi(b, h, j):
                n = turn_pos(h, j)
                act.wait_ge(ring_ready, ring(b, n))
                act.activation(pt_hi[:, j, :], TB[n % 2], ACT.Copy).then_inc(pt_hi_done, 1)

            def lower_half(b, h):
                act.wait_ge(pv_ready, b * H + h + 1)
                act.activation(c32[:, :], PVB[D:P, :], ACT.Copy).then_inc(c_done, 1)

            def result_hi(b, pair):
                act.wait_ge(pv_free, b * H + 2 * pair + 3)
                act.activation(a_hi[:, pair, :], a32[:, pair % 2, :], ACT.Copy).then_inc(ahi_done, 1)

            def v_his(b, t, bank):
                act.wait_ge(v_ready, b * ST + t + 1)
                act.activation(v_sb[:, t, :, 0, :], bank.rearrange("p (h d) -> p h d", d=D), ACT.Copy)\
                    .then_inc(v_hi, 1)

            def weights_split(m):
                act.wait_ge(wraw_loaded[m % 2], 48 * (m // 2 + 1))
                for j in range(3):
                    a = act.activation(w_ff[:, m, 2 * j, :], w_raw[:, m % 2, j, :], ACT.Copy, bias=-ZERO_POINT)
                a.then_inc(whi_done, 1)

            act.wait_ge(bias_ready, 4)
            split_hi(0)
            split_hi(1)
            act.wait_ge(mod_col, 2)
            for f in range(KT):
                modulate(0, f, TB[f % 2])
            split_hi(2)
            proj_hi(0, 0, 0)
            v_his(0, 0, TB[0])
            proj_hi(0, 0, 1)
            k_copy(0, 0)
            v_his(0, 1, TB[1])
            for st in range(ST):
                exps(0, 0, st)
            proj_hi(0, 1, 0)
            v_his(0, 2, TB[0])
            split_hi(3)
            proj_hi(0, 1, 1)
            k_copy(0, 1)
            v_his(0, 3, TB[1])

            def slot(b, h, more):
                after = (b, h + 1) if h < H - 1 else (b + 1, 0)
                last = h == H - 1 and not more
                fill = h < 4 or more
                nxt, pair, qk = filler_of(h)
                weights_hi(b, h, 0)
                weights_hi(b, h, 1)
                if not last:
                    exps(*after, 0)
                    exps(*after, 1)
                    exps(*after, 2)
                    exps(*after, 3)
                weights_hi(b, h, 2)
                if h:
                    lower_half(b, h - 1)
                weights_hi(b, h, 3)
                if fill:
                    proj_hi(b + nxt, pair, qk)
                if fill and qk:
                    k_copy(b + nxt, pair)
                if h and h % 2 == 0:
                    result_hi(b, h // 2 - 1)

            def norm_slot(b, h, more):
                after = (b, h + 1)
                nxt, pair, qk = filler_of(h)
                kind, col = (0, None) if more else (2, 0)
                weights_hi(b, h, 0)
                exps(*after, 0)
                exps(*after, 1)
                modulate(b + 1, 0, PJ, kind, col)
                weights_hi(b, h, 1)
                exps(*after, 2)
                exps(*after, 3)
                modulate(b + 1, 1, PJ, kind, col)
                weights_hi(b, h, 2)
                modulate(b + 1, 2, PJ, kind, col)
                lower_half(b, h - 1)
                weights_hi(b, h, 3)
                modulate(b + 1, 3, PJ, kind, col)
                if more:
                    proj_hi(b + nxt, pair, qk)
                result_hi(b, h // 2 - 1)

            def attention(b, more):
                for h in range(H):
                    (norm_slot if h == 4 else slot)(b, h, more)
                if not more:
                    act.wait_ge(fs_step, 2)
                    weights_split(0)
                lower_half(b, H - 1)
                result_hi(b, PAIRS - 1)
                if more:
                    v_his(b + 1, 0, SC[0])
                for t in range(1, ST if more else 0):
                    v_his(b + 1, t, SC[t])
                if not more:
                    weights_split(1)

            with act.Fori(0, B - 1) as b:
                attention(b, True)
            attention(B - 1, False)

            def squares(m):
                act.wait_ge(wlo_done, m + 1)
                for j in range(3):
                    if m or j:
                        act.wait_ge(squares_done, 3 * m + j)
                    act.activation(lo_square[:, :], w_ff[:, m, 2 * j + 1, :].bitcast(F32), ACT.Square,
                                   accum_out=lo_sums[:, 3 * m + j:3 * m + j + 1]).then_inc(squares_done, 1)

            def ff_modulate(b, f, bank):
                act.activation(h32[:, f % 2, :], bank, ACT.Identity, bias=modc[:, 2, f, bass.ds(b + 1, 1)],
                               scale=modc[:, 3, f, bass.ds(b + 1, 1)]).then_inc(f32_done, 1)

            G = [psum[:, 0, :], psum[:, 2, :]]
            U = [psum[:, 1, :], psum[:, 3, :]]

            def feed_forward(b, bi, more):
                for m in range(MT):
                    if bi == 0 and 2 <= m + 1 < MT:
                        weights_split(m + 1)
                    if m == MT - 1 and more:
                        act.wait_ge(fn_turned, b * 3 + 1)
                        if bi:
                            act.wait_ge(fh_done23, b * 2)
                        else:
                            act.wait_ge(h_done, (B + 1) * KT)
                        ff_modulate(b, 0, G[0])
                        ff_modulate(b, 1, U[0])
                    act.wait_ge(unit_ready, b * MT + m + 1)
                    act.activation(tanh_sb[:, :], G[pair_of(m)], ACT.Tanh, scale=sg_half[:, m:m + 1])\
                        .then_inc(tanh_done, 1)
                    if m == MT - 1 and more:
                        act.wait_ge(f32_done, b * KT + 2)
                        for f in range(2):
                            act.activation(hT_hi[:, f, :], h32[:, f, :], ACT.Copy).then_inc(fh_hi01, 1)
                    act.wait_ge(unit_free, b * MT + m + 1)
                    if bi or m >= 2:
                        act.wait_ge(d_done, b * MT + max(m - 1, 0))
                    act.activation(g_hi[:, m % 2, :], g32[:, :], ACT.Copy).then_inc(ghi_done, 1)
                    if bi == 0:
                        squares(m)
                if more:
                    for f in (2, 3):
                        act.wait_ge(fn_turned, b * 3 + f)
                        act.wait_ge(fh_done01, b * 2 + f - 1)
                        ff_modulate(b, f, G[f - 2])

            feed_forward(0, 0, True)
            with act.Fori(1, B - 1) as b:
                feed_forward(b, 1, True)
            feed_forward(B - 1, B - 1, False)


        @block.vector
        def _(dve):
            def norm_stats(b, t):
                if t == 0:
                    dve.wait_ge(xn_loaded, b * 16 + 16)
                dve.bn_stats(stats[:, t, :], xn[:, t, :]).then_inc(bn_done, 1)

            def norm_aggr(b):
                dve.wait_ge(bn_done, b * ST + ST)
                dve.sem_inc(aggr_begun, 1)
                for t in range(ST):
                    dve.bn_aggr(mv[:, t, :], stats[:, t, :]).then_inc(aggr_done, 1)

            def norm_scale(b, t):
                if t == 0:
                    dve.wait_ge(rstd_done, b + 1)
                dve.tensor_scalar(xn[:, t, :], xn[:, t, :], mv[:, t, 0:1], rstd[:, t:t + 1],
                                  ALU.subtract, ALU.mult).then_inc(ln_done, 1)

            def norm_tokens(b):
                for t in range(ST):
                    norm_stats(b, t)
                norm_aggr(b)
                for t in range(ST):
                    norm_scale(b, t)

            def norm_hi(b, f):
                dve.wait_ge(h32_done, b * KT + f + 1)
                dve.tensor_copy(hT_hi[:, f, :], h32[:, f % 2, :]).then_inc(h_hi, 1)

            dve.wait_ge(silu_step, 1)
            dve.scalar_tensor_tensor(c_silu[:, :, :], c_th[:, :, :], 1.0, c_sb[:, :, :], ALU.add, ALU.mult)\
                .then_inc(silu_step, 1)
            dve.wait_ge(silu_step, 2)
            dve.tensor_scalar(c_silu[:, :, :], c_silu[:, :, :], 0.5, None, ALU.mult).then_inc(silu_step, 1)
            norm_tokens(0)
            dve.wait_ge(bias_ready, 2)
            dve.tensor_tensor(bo_lo[:, :], bo_f, bo_hi[:, :].bitcast(F32), ALU.subtract).then_inc(bias_ready, 1)
            dve.tensor_copy(ones_r[:, :], ones_f[:, :]).then_inc(bias_ready, 1)

            def mod_columns(kind, n):
                dve.wait_ge(mod_mm, n)
                turned = SC[COLS[kind]][:, 0:KT * B].rearrange("p (k b) -> p k b", b=B)
                dve.tensor_scalar(modc[:, COLS[kind], :, :], turned, float(kind in (CA, CB)), None, ALU.add)\
                    .then_inc(mod_col, 1)

            def gate(g, n):
                bank = PVB[0:B, :]
                dve.wait_ge(mod_mm, n)
                dve.tensor_scalar(g_tmp[0:B, 0, :], bank, 0.0, 2.0, ALU.is_ge, ALU.mult).then_inc(gate_step, 1)
                dve.tensor_scalar(g_tmp[0:B, 1, :], bank, -1.0, 0.25, ALU.mult, ALU.max).then_inc(gate_step, 1)
                dve.wait_ge(gate_step, 3 * g + 2)
                dve.tensor_tensor(g_tmp[0:B, 1, :], bank, g_tmp[0:B, 1, :], ALU.max).then_inc(gate_step, 1)
                dve.wait_ge(gate_step, 3 * g + 3)
                dve.scalar_tensor_tensor(g_rows[g], g_tmp[0:B, 0, :], -1.0, g_tmp[0:B, 1, :],
                                         ALU.add, ALU.mult).then_inc(gate_rows, 1)

            def split_lo(w):
                dve.wait_ge(w_hi_done, w + 1)
                dve.scalar_tensor_tensor(W_lo[w].rearrange("p k n -> p (k n)"),
                                         w_stage[w].rearrange("p k n -> p (k n)"),
                                         QSCALE if w == 0 else 1.0,
                                         W_hi[w].bitcast(F32).rearrange("p k n -> p (k n)"),
                                         ALU.mult, ALU.subtract).then_inc(w_lo_done, 1)

            def proj_lo(b, pair, qk):
                dve.wait_ge(pj_hi, b * H + 2 * pair + qk + 1)
                for w, src, other in ((0, slice(0, D), slice(D, P)), (1, slice(D, P), slice(0, D))):
                    hi = (qs, kh)[qk][src, pair % 2, w, :].bitcast(F32)
                    dst = qs[other, pair % 2, w, :] if qk == 0 else kl[src, pair % 2, :]
                    d = dve.scalar_tensor_tensor(dst, PJ[src, :], bqkv[src, qk, pair:pair + 1], hi,
                                                 ALU.add, ALU.subtract)
                d.then_inc(pj_done, 1)

            def row_maxima(b, h, st):
                dve.wait_ge(s_ready, b * 32 + 4 * h + st + 2)
                dve.tensor_reduce(negmax[:, h % 2, st:st + 2], psum[:, st:st + 2, :], AXX, ALU.max, negate=True)\
                    .then_inc(max_done, 1)

            def row_recips(b, h, st):
                dve.wait_ge(exp_done, b * 32 + 4 * h + st + 2)
                dve.reciprocal(rinv[:, h % 2, st:st + 2], ssum[:, h % 2, st:st + 2]).then_inc(rinv_done, 1)

            def weights_lo(b, h, j):
                dve.wait_ge(pt_hi_done, b * 32 + 4 * h + j + 1)
                dve.tensor_tensor(pt_lo[:, j, :], TB[turn_pos(h, j) % 2], pt_hi[:, j, :].bitcast(F32),
                                  ALU.subtract).then_inc(ring_free, 1)

            def join_halves(b, h):
                dve.wait_ge(c_done, b * H + h + 1)
                rows_ = slice(D * (h % 2), D * (h % 2) + D)
                dve.scalar_tensor_tensor(a32[rows_, h // 2 % 2, :], PVB[0:D, :], bv_h[:, h:h + 1], c32[:, :],
                                         ALU.add, ALU.add).then_inc(pv_free, 1)

            def v_los(b, t, bank):
                dve.wait_ge(v_hi, b * ST + t + 1)
                dve.tensor_tensor(v_sb[:, t, :, 1, :], bank.rearrange("p (h d) -> p h d", d=D),
                                  v_sb[:, t, :, 0, :].bitcast(F32), ALU.subtract).then_inc(v_done, 1)

            def split_lo_b(m):
                dve.wait_ge(whi_done, m + 1)
                for j in range(3):
                    d = dve.scalar_tensor_tensor(w_ff[:, m, 2 * j + 1, :], w_raw[:, m % 2, j, :], -ZERO_POINT,
                                                 w_ff[:, m, 2 * j, :].bitcast(F32), ALU.add, ALU.subtract)
                d.then_inc(wlo_done, 1)

            dve.sem_inc(ring_free, 2)
            dve.sem_inc(pv_free, 1)
            dve.sem_inc(y_done, ST)
            mod_columns(SA, 1)
            split_lo(0)
            mod_columns(CA, 2)
            split_lo(1)
            for f in range(KT):
                norm_hi(0, f)
            split_lo(2)
            proj_lo(0, 0, 0)
            v_los(0, 0, TB[0])
            proj_lo(0, 0, 1)
            v_los(0, 1, TB[1])
            row_maxima(0, 0, 0)
            row_maxima(0, 0, 2)
            row_recips(0, 0, 0)
            row_recips(0, 0, 2)
            proj_lo(0, 1, 0)
            dve.wait_ge(h_done, KT)
            gate(0, 3)
            v_los(0, 2, TB[0])
            split_lo(3)
            proj_lo(0, 1, 1)
            norm_tokens(1)
            mod_columns(SB, 4)
            mod_columns(CB, 5)
            gate(1, 6)
            v_los(0, 3, TB[1])
            dve.wait_ge(fs_loaded, 32)
            dve.scalar_tensor_tensor(sgu_half[:, :], sg_half[:, :], 0.5, su_col[:, :], ALU.mult, ALU.mult)\
                .then_inc(fs_step, 1)
            dve.wait_ge(fs_step, 1)
            dve.tensor_scalar(sg_half[:, :], sg_half[:, :], 0.5, None, ALU.mult).then_inc(fs_step, 1)

            def slot(b, h, more):
                after = (b, h + 1) if h < H - 1 else (b + 1, 0)
                last = h == H - 1 and not more
                fill = h < 4 or more
                nxt, pair, qk = filler_of(h)
                if not last:
                    row_maxima(*after, 0)
                    row_maxima(*after, 2)
                weights_lo(b, h, 0)
                if not last:
                    row_recips(*after, 0)
                weights_lo(b, h, 1)
                if not last:
                    row_recips(*after, 2)
                weights_lo(b, h, 2)
                if h:
                    join_halves(b, h - 1)
                weights_lo(b, h, 3)
                if fill:
                    proj_lo(b + nxt, pair, qk)

            def norm_slot(b, h, more):
                after = (b, h + 1)
                nxt, pair, qk = filler_of(h)
                row_maxima(*after, 0)
                row_maxima(*after, 2)
                row_recips(*after, 0)
                norm_hi(b + 1, 0)
                weights_lo(b, h, 0)
                row_recips(*after, 2)
                norm_hi(b + 1, 1)
                weights_lo(b, h, 1)
                weights_lo(b, h, 2)
                norm_hi(b + 1, 2)
                join_halves(b, h - 1)
                weights_lo(b, h, 3)
                norm_hi(b + 1, 3)
                if more:
                    proj_lo(b + nxt, pair, qk)

            def attention(b, later):
                more = later > 0
                for h in range(H):
                    (norm_slot if h == 4 else slot)(b, h, more)
                join_halves(b, H - 1)
                if more:
                    v_los(b + 1, 0, SC[0])
                for t in range(1, ST if more else 0):
                    if later:
                        norm_stats(b + 2, t - 1)
                    v_los(b + 1, t, SC[t])
                if later:
                    norm_stats(b + 2, ST - 1)
                    norm_aggr(b + 2)
                if not more:
                    split_lo_b(0)
                    split_lo_b(1)
                dve.wait_ge(gate_loaded, b * 16 + 16)
                for s in range(ST):
                    n = out_pos(s)
                    dve.wait_ge(ring_ready, ring(b, n))
                    dve.wait_ge(x_done, b * ST + s + 1)
                    dve.tensor_tensor(t32[:, s % 2, :], TB[n % 2], gate_bc[:, :], ALU.mult).then_inc(ring_free, 1)
                    if later:
                        norm_scale(b + 2, s)

            with dve.Fori(0, B - 2) as b:
                attention(b, 2)
            attention(B - 2, 1)
            attention(B - 1, 0)

            G = [psum[:, 0, :], psum[:, 2, :]]
            U = [psum[:, 1, :], psum[:, 3, :]]
            Y = [psum[:, 4 + s, :] for s in range(ST)]

            def weights_flag():
                dve.wait_ge(squares_done, 3 * MT)
                dve.tensor_reduce(lo_sum[:, :], lo_sums[:, :], AXX, ALU.max).then_inc(lo_summed, 1)
                dve.wait_ge(lo_turned, 16)
                dve.tensor_reduce(lo_all[:, :], lo_row[:, :], AXX, ALU.max).then_inc(lo_summed, 1)
                dve.wait_ge(lo_summed, 2)
                dve.tensor_scalar(lo_flag[:, :], lo_all[:, :], 0.0, None, ALU.is_gt).then_inc(lo_known, 1)

            def feed_forward(b, bi, more):
                for m in range(MT):
                    if bi == 0 and 2 <= m + 1 < MT:
                        split_lo_b(m + 1)
                    u = pair_of(m)
                    dve.wait_ge(tanh_done, b * MT + m + 1)
                    dve.scalar_tensor_tensor(a_sb[:, :], tanh_sb[:, :], 1.0, G[u], ALU.add, ALU.mult)\
                        .then_inc(a_step, 1)
                    dve.wait_ge(a_step, b * MT + m + 1)
                    dve.scalar_tensor_tensor(g32[:, :], U[u], sgu_half[:, m:m + 1], a_sb[:, :],
                                             ALU.mult, ALU.mult).then_inc(unit_free, 1)
                    dve.wait_ge(ghi_done, b * MT + m + 1)
                    dve.tensor_tensor(g_lo[:, m % 2, :], g32[:, :], g_hi[:, m % 2, :].bitcast(F32),
                                      ALU.subtract).then_inc(g_done, 1)
                    if more:
                        for t in {2: (0,), 3: (1,), 4: (2, 3)}.get(m, ()):
                            norm_stats(b + B + 1, t)
                        if m == 4:
                            norm_aggr(b + B + 1)
                        if 5 <= m < 9:
                            norm_scale(b + B + 1, m - 5)
                    if bi == 0 and m == MT - 1:
                        weights_flag()
                for f in (2, 3) if more else ():
                    dve.wait_ge(f32_done, b * KT + f + 1)
                    dve.tensor_copy(hT_hi[:, f, :], h32[:, f % 2, :]).then_inc(fh_hi23, 1)
                    dve.wait_ge(fh_hi23, b * 2 + f - 1)
                    dve.tensor_tensor(hT_lo[:, f, :], h32[:, f % 2, :], hT_hi[:, f, :].bitcast(F32),
                                      ALU.subtract).then_inc(fh_done23, 1)
                dve.wait_ge(gs_done, b + 1)
                dve.wait_ge(d_done, b * MT + MT)
                for s in range(ST):
                    dve.wait_ge(fx_done, b * ST + s + 1)
                    dve.tensor_tensor(t32[:, s % 2, :], Y[s], gate_bc[:, :], ALU.mult).then_inc(y_done, 1)

            feed_forward(0, 0, True)
            with dve.Fori(1, B - 1) as b:
                feed_forward(b, 1, True)
            feed_forward(B - 1, B - 1, False)

        @block.gpsimd
        def _(pool):
            pool.memset(ident[:, :], 0.0).then_inc(ln_step, 1)
            pool.memset(neg_half[:, :], -0.5).then_inc(ln_step, 1)
            pool.memset(ones_f[:, :], 1.0).then_inc(ln_step, 1)
            pool.memset(eps_t[:, :], EPS).then_inc(ln_step, 1)
            pool.memset(three_halves[:, :], 1.5).then_inc(ln_step, 1)
            pool.wait_ge(ln_step, 5)
            pool.affine_select(out=ident[:, :], in_=ident[:, :], compare_op=ALU.not_equal, fill=1.0, base=0,
                               pattern=[[-1, P]], channel_multiplier=1).then_inc(const_ready, 1)
            pool.sem_inc(x_done, 2)
            pool.sem_inc(fx_done, 2)

            def inv_std(b):
                def after(k):
                    pool.wait_ge(ln_step, b * 6 + 5 + k)

                pool.wait_ge(aggr_done, b * ST + ST)
                pool.tensor_tensor(veps[:, :], mv[:, :, 1], eps_t[:, :], ALU.add).then_inc(ln_step, 1)
                after(1)
                pool.tensor_tensor(rstd[:, :], veps[:, :], neg_half[:, :], ALU.pow).then_inc(ln_step, 1)
                after(2)
                pool.tensor_tensor(newt[:, :], rstd[:, :], rstd[:, :], ALU.mult).then_inc(ln_step, 1)
                after(3)
                pool.tensor_tensor(newt[:, :], newt[:, :], veps[:, :], ALU.mult).then_inc(ln_step, 1)
                after(4)
                pool.tensor_tensor(newt[:, :], newt[:, :], neg_half[:, :], ALU.mult).then_inc(ln_step, 1)
                after(5)
                pool.tensor_tensor(newt[:, :], newt[:, :], three_halves[:, :], ALU.add).then_inc(ln_step, 1)
                after(6)
                pool.tensor_tensor(rstd[:, :], rstd[:, :], newt[:, :], ALU.mult).then_inc(rstd_done, 1)

            def divide(b, h, st):
                if st % 2 == 0:
                    pool.wait_ge(rinv_done, b * 16 + 2 * h + st // 2 + 1)
                row = pr[:, h % 2, st, :]
                pool.tensor_tensor(row, row, rinv[:, h % 2, st:st + 1].to_broadcast([P, S]), ALU.mult)\
                    .then_inc(p_done, 1)

            def norm_lo(b, f):
                pool.wait_ge(h_hi, b * KT + f + 1)
                pool.tensor_tensor(hT_lo[:, f, :], h32[:, f % 2, :], hT_hi[:, f, :].bitcast(F32),
                                   ALU.subtract).then_inc(h_done, 1)

            def result_lo(b, pair):
                pool.wait_ge(ahi_done, b * PAIRS + pair + 1)
                pool.tensor_tensor(a_lo[:, pair, :], a32[:, pair % 2, :], a_hi[:, pair, :].bitcast(F32),
                                   ALU.subtract).then_inc(a_done, 1)

            inv_std(0)
            for f in range(KT):
                norm_lo(0, f)
            for st in range(ST):
                divide(0, 0, st)
            inv_std(1)

            def slot(b, h, more):
                after = (b, h + 1) if h < H - 1 else (b + 1, 0)
                last = h == H - 1 and not more
                if not last:
                    divide(*after, 0)
                    divide(*after, 1)
                    divide(*after, 2)
                    divide(*after, 3)
                if h and h % 2 == 0:
                    result_lo(b, h // 2 - 1)

            def norm_slot(b, h, more):
                after = (b, h + 1)
                divide(*after, 0)
                divide(*after, 1)
                norm_lo(b + 1, 0)
                norm_lo(b + 1, 1)
                norm_lo(b + 1, 2)
                norm_lo(b + 1, 3)
                divide(*after, 2)
                divide(*after, 3)
                result_lo(b, h // 2 - 1)

            def attention(b, later):
                more = later > 0
                for h in range(H):
                    (norm_slot if h == 4 else slot)(b, h, more)
                result_lo(b, PAIRS - 1)
                if later:
                    inv_std(b + 2)
                pool.wait_ge(xr_loaded, b * 16 + 16)
                for s in range(ST):
                    pool.wait_ge(ring_free, ring(b, out_pos(s)) + 2)
                    pool.tensor_tensor(xr[:, s, :], xr[:, s, :], t32[:, s % 2, :], ALU.add).then_inc(x_done, 1)

            with pool.Fori(0, B - 2) as b:
                attention(b, 2)
            attention(B - 2, 1)
            attention(B - 1, 0)

            pool.wait_ge(sdown_loaded, 16)

            def feed_forward(b, more):
                pool.wait_ge(fg_loaded, b * 16 + 16)
                pool.tensor_tensor(gate_bc[:, :], gate_bc[:, :], sdown_bc[:, :], ALU.mult).then_inc(gs_done, 1)
                if more:
                    inv_std(b + B + 1)
                    for f in range(2):
                        pool.wait_ge(fh_hi01, b * 2 + f + 1)
                        pool.tensor_tensor(hT_lo[:, f, :], h32[:, f, :], hT_hi[:, f, :].bitcast(F32),
                                           ALU.subtract).then_inc(fh_done01, 1)
                pool.wait_ge(fr_loaded, b * 16 + 16)
                for s in range(ST):
                    pool.wait_ge(y_done, b * ST + ST + s + 1)
                    pool.tensor_tensor(xr[:, s, :], xr[:, s, :], t32[:, s % 2, :], ALU.add).then_inc(fx_done, 1)

            with pool.Fori(0, B - 1) as b:
                feed_forward(b, True)
            feed_forward(B - 1, False)


def kernel(L0_attn_x, L0_attn_Wq, L0_attn_bq, L0_attn_Wk, L0_attn_bk, L0_attn_Wv, L0_attn_bv, L0_attn_Wo,
           L0_attn_bo, L0_ffn_wq_gate, L0_ffn_s_gate, L0_ffn_wq_up, L0_ffn_s_up, L0_ffn_wq_down, L0_ffn_s_down,
           L0_c, L0_wmod):
    import numpy as np
    import concourse.bacc as bacc
    from concourse.bass_utils import run_bass_kernel_spmd

    def tiles_in(w):
        return np.asarray(w).reshape(MT, P, KT, P).transpose(0, 3, 2, 1).reshape(MT, P, F)

    arrays = {
        "x": L0_attn_x,
        "c_t": np.asarray(L0_c).T,
        "wmod": L0_wmod,
        "w_q": L0_attn_Wq, "w_k": L0_attn_Wk, "w_v": L0_attn_Wv, "w_o": L0_attn_Wo,
        "b_q": np.asarray(L0_attn_bq).reshape(PAIRS, P).T,
        "b_k": np.asarray(L0_attn_bk).reshape(PAIRS, P).T,
        "b_v": np.asarray(L0_attn_bv).reshape(H, D).T,
        "b_o": np.asarray(L0_attn_bo).reshape(1, F),
        "w_gate": tiles_in(L0_ffn_wq_gate),
        "w_up": tiles_in(L0_ffn_wq_up),
        "w_down": np.asarray(L0_ffn_wq_down).reshape(F, MT, P).transpose(1, 2, 0),
        "s_gate": np.asarray(L0_ffn_s_gate).reshape(MT, P).T,
        "s_up": np.asarray(L0_ffn_s_up).reshape(MT, P).T,
        "s_down": np.asarray(L0_ffn_s_down).reshape(1, F),
    }
    arrays = {n: np.ascontiguousarray(a) for n, a in arrays.items()}
    nc = bacc.Bacc("TRN2", target_bir_lowering=False, num_devices=1)
    args = {n: nc.dram_tensor(n, a.shape, mybir.dt.from_np(a.dtype), kind="ExternalInput").ap()
            for n, a in arrays.items()}
    out = nc.dram_tensor("out", (B, S, F), F32, kind="ExternalOutput").ap()
    adaln_block(nc, **args, out=out)
    r = run_bass_kernel_spmd(nc, [arrays], core_ids=[0])
    return r.results[0]["out"]
```
